# Optimizing a Trainium2 kernel written in Bass

```python
import numpy as np
import jax
import jax.numpy as jnp

def _softmax(x, axis=-1):
    return jax.nn.softmax(x, axis=axis)

def _gelu(x):
    return jax.nn.gelu(x, approximate=True)

def _silu(x):
    return jax.nn.silu(x)

def _sigmoid(x):
    return jax.nn.sigmoid(x)

def _layernorm(x, axis=-1, eps=1e-05):
    m = jnp.mean(x, axis=axis, keepdims=True)
    v = jnp.var(x, axis=axis, keepdims=True)
    return (x - m) / jnp.sqrt(v + eps)

def _scatter_add(tgt, idx, src, axis=0):
    return tgt.at[idx].add(src)

def _segment_sum(src, seg, n):
    return jax.ops.segment_sum(src, seg, n)
kernel_name = 'mk_seq_postln_d1_jaxref_r8_69b791'

def setup_inputs(seed: int=0):
    np.random.seed(seed)
    _w = jnp.asarray

    def _L0_attn_setup():
        import jax, jax.numpy as jnp
        import numpy as np
        B, T, C = (1, 256, 256)
        N_HEADS, N_KV_HEADS = (32, 8)
        D_HEAD = C // N_HEADS
        WINDOW = 64
        ROPE_BASE = 10000.0

        def _rope_tables(seq_len, d_head, dtype):
            inv_freq = 1.0 / ROPE_BASE ** (jnp.arange(0, d_head, 2, dtype=jnp.float32) / d_head)
            t = jnp.arange(seq_len, dtype=jnp.float32)
            freqs = t[:, None] * inv_freq[None, :]
            emb = jnp.concatenate([freqs, freqs], axis=-1)
            return (jnp.cos(emb).astype(dtype), jnp.sin(emb).astype(dtype))

        def _rotate_half(u):
            d = u.shape[-1]
            return jnp.concatenate([-u[..., d // 2:], u[..., :d // 2]], axis=-1)
        key = jax.random.key(seed)
        ks = jax.random.split(key, 5)
        s = 0.02
        return {'x': jax.random.normal(ks[0], (B, T, C), dtype=jnp.float32), 'wq': jax.random.normal(ks[1], (C, N_HEADS * D_HEAD), dtype=jnp.float32) * s, 'wk': jax.random.normal(ks[2], (C, N_KV_HEADS * D_HEAD), dtype=jnp.float32) * s, 'wv': jax.random.normal(ks[3], (C, N_KV_HEADS * D_HEAD), dtype=jnp.float32) * s, 'wo': jax.random.normal(ks[4], (N_HEADS * D_HEAD, C), dtype=jnp.float32) * s}
    _L0_attn_in = _L0_attn_setup()

    def _L0_ffn_setup():
        import jax, jax.numpy as jnp
        import numpy as np
        ALPHA = 1.702
        LIMIT = 7.0
        TOP_K = 4
        B, S, H = (1, 128, 256)
        E, D = (16, 256)
        key = jax.random.key(seed)
        ks = jax.random.split(key, 7)
        s = 0.02
        return {'hidden_states': jax.random.normal(ks[0], (B, S, H), dtype=jnp.float32), 'router_weight': jax.random.normal(ks[1], (E, H), dtype=jnp.float32) * s, 'router_bias': jax.random.normal(ks[2], (E,), dtype=jnp.float32) * s, 'gate_up_proj': jax.random.normal(ks[3], (E, H, 2 * D), dtype=jnp.float32) * s, 'gate_up_proj_bias': jax.random.normal(ks[4], (E, 2 * D), dtype=jnp.float32) * s, 'down_proj': jax.random.normal(ks[5], (E, D, H), dtype=jnp.float32) * s, 'down_proj_bias': jax.random.normal(ks[6], (E, H), dtype=jnp.float32) * s}
    _L0_ffn_in = _L0_ffn_setup()
    _d = {'L0_attn_x': _L0_attn_in['x'], 'L0_attn_wq': _L0_attn_in['wq'], 'L0_attn_wk': _L0_attn_in['wk'], 'L0_attn_wv': _L0_attn_in['wv'], 'L0_attn_wo': _L0_attn_in['wo'], 'L0_ffn_router_weight': _L0_ffn_in['router_weight'], 'L0_ffn_router_bias': _L0_ffn_in['router_bias'], 'L0_ffn_gate_up_proj': _L0_ffn_in['gate_up_proj'], 'L0_ffn_gate_up_proj_bias': _L0_ffn_in['gate_up_proj_bias'], 'L0_ffn_down_proj': _L0_ffn_in['down_proj'], 'L0_ffn_down_proj_bias': _L0_ffn_in['down_proj_bias']}
    _x0 = _d['L0_attn_x']
    _d['L0_attn_x'] = jax.random.normal(jax.random.fold_in(jax.random.key(seed), 1), (1, 1024, 256), dtype=_x0.dtype)
    del _x0
    return _d

def reference(L0_attn_x, L0_attn_wq, L0_attn_wk, L0_attn_wv, L0_attn_wo, L0_ffn_router_weight, L0_ffn_router_bias, L0_ffn_gate_up_proj, L0_ffn_gate_up_proj_bias, L0_ffn_down_proj, L0_ffn_down_proj_bias):

    def _L0_attn_ref(x, wq, wk, wv, wo):
        import jax, jax.numpy as jnp
        import numpy as np
        B, T, C = (1, 256, 256)
        N_HEADS, N_KV_HEADS = (32, 8)
        D_HEAD = C // N_HEADS
        WINDOW = 64
        ROPE_BASE = 10000.0

        def _rope_tables(seq_len, d_head, dtype):
            inv_freq = 1.0 / ROPE_BASE ** (jnp.arange(0, d_head, 2, dtype=jnp.float32) / d_head)
            t = jnp.arange(seq_len, dtype=jnp.float32)
            freqs = t[:, None] * inv_freq[None, :]
            emb = jnp.concatenate([freqs, freqs], axis=-1)
            return (jnp.cos(emb).astype(dtype), jnp.sin(emb).astype(dtype))

        def _rotate_half(u):
            d = u.shape[-1]
            return jnp.concatenate([-u[..., d // 2:], u[..., :d // 2]], axis=-1)
        b, t, c = x.shape
        n_rep = N_HEADS // N_KV_HEADS
        q = (x @ wq).reshape(b, t, N_HEADS, D_HEAD)
        k = (x @ wk).reshape(b, t, N_KV_HEADS, D_HEAD)
        v = (x @ wv).reshape(b, t, N_KV_HEADS, D_HEAD)
        cos, sin = _rope_tables(t, D_HEAD, x.dtype)
        cos = cos[None, :, None, :]
        sin = sin[None, :, None, :]
        q = q * cos + _rotate_half(q) * sin
        k = k * cos + _rotate_half(k) * sin
        k = jnp.repeat(k, n_rep, axis=2)
        v = jnp.repeat(v, n_rep, axis=2)
        scale = 1.0 / np.sqrt(D_HEAD)
        scores = jnp.einsum('bqhd,bkhd->bhqk', q, k) * scale
        qi = jnp.arange(t)[:, None]
        ki = jnp.arange(t)[None, :]
        allowed = (ki <= qi) & (qi - ki <= WINDOW)
        scores = jnp.where(allowed[None, None, :, :], scores, -jnp.inf)
        attn = jax.nn.softmax(scores, axis=-1)
        out = jnp.einsum('bhqk,bkhd->bqhd', attn, v).reshape(b, t, N_HEADS * D_HEAD)
        return out @ wo

    def _L0_ffn_ref(hidden_states, router_weight, router_bias, gate_up_proj, gate_up_proj_bias, down_proj, down_proj_bias):
        import jax, jax.numpy as jnp
        import numpy as np
        ALPHA = 1.702
        LIMIT = 7.0
        TOP_K = 4
        B, S, H = (1, 128, 256)
        E, D = (16, 256)
        batch, seq, hdim = hidden_states.shape
        x = hidden_states.reshape(-1, hdim)
        T = x.shape[0]
        logits = x @ router_weight.T + router_bias
        top_val, top_idx = jax.lax.top_k(logits, TOP_K)
        top_val = jax.nn.softmax(top_val, axis=-1)
        router_scores = jnp.zeros_like(logits).at[jnp.arange(T)[:, None], top_idx].set(top_val)
        gate_up = jnp.einsum('th,ehd->etd', x, gate_up_proj) + gate_up_proj_bias[:, None, :]
        gate = gate_up[..., ::2]
        up = gate_up[..., 1::2]
        gate = jnp.minimum(gate, LIMIT)
        up = jnp.clip(up, -LIMIT, LIMIT)
        glu = gate * jax.nn.sigmoid(gate * ALPHA)
        out = jnp.einsum('etd,edh->eth', (up + 1.0) * glu, down_proj) + down_proj_bias[:, None, :]
        out = out * router_scores.T[:, :, None]
        out = out.sum(axis=0)
        return out.reshape(batch, seq, hdim)
    x = L0_attn_x
    x = _layernorm(x + _L0_attn_ref(x, L0_attn_wq, L0_attn_wk, L0_attn_wv, L0_attn_wo), axis=-1)
    x = _layernorm(x + _L0_ffn_ref(x, L0_ffn_router_weight, L0_ffn_router_bias, L0_ffn_gate_up_proj, L0_ffn_gate_up_proj_bias, L0_ffn_down_proj, L0_ffn_down_proj_bias), axis=-1)
    return x

_drawn_inputs = setup_inputs


def setup_inputs(seed=0):
    import zlib

    import numpy as np

    out = dict(_drawn_inputs(seed))
    spreads = {}
    factors = {'L0_attn_wq': 8.0,
     'L0_attn_wk': 8.0,
     'L0_attn_wv': 3.794,
     'L0_attn_wo': 4.004,
     'L0_ffn_router_bias': 8.0,
     'L0_ffn_gate_up_proj_bias': 26.827,
     'L0_ffn_down_proj_bias': 5.555}
    for name, (base, spread) in spreads.items():
        noise = np.random.default_rng([zlib.crc32(name.encode()), seed]).standard_normal(out[name].shape)
        drawn = base * np.exp(spread * noise) if base else spread * noise
        out[name] = jnp.asarray(drawn.astype(out[name].dtype))
    for name, factor in factors.items():
        out[name] = (out[name] * factor).astype(out[name].dtype)
    return out
```

```python
from contextlib import ExitStack

import numpy as np

import concourse.bass as bass
from concourse import mybir

ALU = mybir.AluOpType
ACT = mybir.ActivationFunctionType
AX = mybir.AxisListType
F32 = mybir.dt.float32
F32R = mybir.dt.float32r
BF16 = mybir.dt.bfloat16
I32 = mybir.dt.int32
U32 = mybir.dt.uint32

T, C = 1024, 256
HEADS, KV, DH = 32, 8, 8
WINDOW = 64
REP = HEADS // KV
P = 128
TILES = T // P
Q = 64
CC = C // P
FEAT = 32
GRP = 4
HALVES = KV // GRP
ROW_NEGMAX = 3 * DH
ROW_PAD = 3 * DH + 2
NEG = -1e30
E, D, TOPK = 16, 256, 4
ALPHA, LIMIT = 1.702, 7.0
EPS = 1e-5
ROOT_STEPS = 4
QKV = C + 2 * KV * DH
QK_HEADS = HEADS + KV


def wait_apart(eng, semaphore, value, settled, settled_value):
    eng.wait_ge(settled, settled_value)
    eng.wait_ge(semaphore, value)


def constants():
    inv = (1.0 / 10000.0 ** (np.arange(0, DH, 2, dtype=np.float32) / np.float32(DH))).astype(np.float32)
    ang = np.arange(T, dtype=np.float32)[:, None] * inv[None, :]
    cos, sin = np.cos(ang).astype(np.float32), np.sin(ang).astype(np.float32)
    rope = np.concatenate([cos, cos, -sin, sin], 1).reshape(TILES, P, 2 * DH).transpose(1, 0, 2)
    ident = np.eye(P, dtype=np.float32)
    qi, ki = np.arange(Q)[:, None], np.arange(P)[None, :]
    ok = (ki <= qi + WINDOW) & (ki >= qi)
    mask = np.where(ok, 0.0, NEG).astype(np.float32)
    mask_q = np.tile(np.concatenate([mask, mask], 0), (1, GRP))
    mask_k = np.tile(mask.T, (1, 8))
    group = np.zeros((P, GRP), np.float32)
    for g in range(GRP):
        group[g * FEAT:(g + 1) * FEAT, g] = 1.0
    key_pad = np.zeros((P, KV), np.float32)
    for k in range(KV):
        key_pad[(k % GRP) * FEAT + ROW_PAD, k] = NEG
    lo_row = np.zeros((P, 1), np.float32)
    for g in range(GRP):
        lo_row[g * FEAT + 2 * DH:g * FEAT + 3 * DH] = -1.0
    small = np.concatenate([group, key_pad, lo_row, np.tile(np.arange(E, dtype=np.float32), (P, 1))], 1)
    qk_const = np.zeros((P, QK_HEADS, DH), np.float32)
    qk_const[:, :HEADS, ROW_PAD - 3 * DH] = 1.0
    qk_const[:, HEADS:, 0:2] = 1.0
    return {"c_rope": np.ascontiguousarray(rope), "c_ident": ident, "c_mask": np.stack([mask_q, mask_k]),
            "c_small": small, "c_qk": qk_const}


def build(nc, a, out):
    with ExitStack() as ctx:
        def sb(name, shape, dt=F32):
            return ctx.enter_context(nc.sbuf_tensor(name, shape, dt))

        def sem(name):
            return ctx.enter_context(nc.semaphore(name))

        rope = sb("rope", [P, TILES, 2 * DH])
        ident = sb("ident", [P, P])
        ident_b = sb("ident_b", [P, P], BF16)
        mask_f = sb("mask_f", [P, 2, 512])
        mask = sb("mask", [P, 2, 512], BF16)
        small = sb("small", [P, GRP + KV + 1 + E])
        group_of = small[:, 0:GRP]
        key_pad = small[:, GRP:GRP + KV]
        lo_row = small[:, GRP + KV:GRP + KV + 1]
        expert_no = small[:, GRP + KV + 1:GRP + KV + 1 + E]
        qk_const = sb("qk_const", [P, QK_HEADS, DH])
        x_res = sb("x_res", [P, TILES, C])
        z_res = sb("z_res", [P, TILES, C])
        zT_hi = sb("zT_hi", [P, CC, T], F32R)
        zT_lo = sb("zT_lo", [P, CC, T], F32R)
        logits = sb("logits", [P, TILES, E])
        router = sb("router", [P, CC, E])
        router_b = sb("router_b", [1, E])
        ones_row = sb("ones_row", [1, P])
        w_qkv = sb("w_qkv", [P, CC, QKV])
        w_qkv_hi = sb("w_qkv_hi", [P, CC, QKV], F32R)
        w_qkv_lo = sb("w_qkv_lo", [P, CC, QKV], F32R)
        w_o = sb("w_o", [P, HALVES * REP, C])
        w_o_hi = sb("w_o_hi", [P, HALVES * REP, C], F32R)
        w_o3 = sb("w_o3", [P, HALVES * REP, C], F32R)
        root_consts = sb("root_consts", [P, 4])
        c_eps, c_minus_half, c_minus_one, c_one = (root_consts[:, i:i + 1] for i in range(4))
        down_b = sb("down_b", [E, C])
        up_b = sb("up_b", [P, E, 4])
        w_up = [sb(f"w_up{i}", [P, CC, 2 * D]) for i in range(2)]
        w_up_hi = [sb(f"w_up_hi{i}", [P, CC, 2 * D], F32R) for i in range(2)]
        w_up_lo = [sb(f"w_up_lo{i}", [P, CC, 2 * D], F32R) for i in range(2)]
        w_dn = [sb(f"w_dn{i}", [P, CC, C]) for i in range(2)]
        w_dn_hi = [sb(f"w_dn_hi{i}", [P, CC, C], F32R) for i in range(2)]
        w_dn_lo = [sb(f"w_dn_lo{i}", [P, CC, C], F32R) for i in range(2)]
        shared = ctx.enter_context(ExitStack())

        def sb(name, shape, dt=F32):
            return shared.enter_context(nc.sbuf_tensor(name, shape, dt))

        xT = [sb(f"xT{p}", [P, CC, P]) for p in range(2)]
        xT_hi = [sb(f"xT_hi{p}", [P, CC, P], F32R) for p in range(2)]
        xT_lo = [sb(f"xT_lo{p}", [P, CC, P], F32R) for p in range(2)]
        qk_parts = [sb(f"qk_parts{p}", [P, QK_HEADS, FEAT], F32R) for p in range(2)]
        q_t = [sb(f"q_t{p}", [P, 2, HALVES * REP, Q], F32R) for p in range(2)]
        q_max = [sb(f"q_max{p}", [P, 2, HALVES * REP, Q], F32R) for p in range(2)]
        k_t = [sb(f"k_t{p}", [P, KV, WINDOW + P], F32R) for p in range(2)]
        v_lead = [sb(f"v_lead{p}", [P, KV, FEAT]) for p in range(2)]
        v_own = [sb(f"v_own{p}", [P, KV, FEAT]) for p in range(2)]
        z_tile = [sb(f"z_tile{p}", [P, C]) for p in range(2)]
        rope_a = sb("rope_a", [P, QK_HEADS, DH])
        rope_b = sb("rope_b", [P, QK_HEADS, DH])
        roped = sb("roped", [P, QK_HEADS, DH])
        neg_max = sb("neg_max", [P, 8, GRP])
        max_rows = sb("max_rows", [P, 8, GRP, FEAT], F32R)
        probs = [sb(f"probs{i}", [P, 512]) for i in range(4)]
        o_tok = sb("o_tok", [P, 16, FEAT])
        o_inv = sb("o_inv", [P, 16])
        o_norm = sb("o_norm", [P, 16, DH])
        o_parts = sb("o_parts", [P, 16, FEAT], F32R)
        o_back = [sb(f"o_back{i}", [P, 16 * FEAT]) for i in range(2)]
        o_t = sb("o_t", [P, HALVES * REP, P], F32R)
        resid = sb("resid", [P, C])
        stats = sb("stats", [P, 6])
        mean_var = sb("mean_var", [P, 2])
        var_eps = sb("var_eps", [P, 1])
        rstd = sb("rstd", [P, 1])
        shift = sb("shift", [P, 1])
        mean_rstd = sb("mean_rstd", [P, 1])
        zT_own = sb("zT_own", [P, CC, P])

        bank = [ctx.enter_context(nc.psum_tensor(f"bank{i}", [P, 512], F32)) for i in range(8)]
        b_mix, b_qt, b_o, b_s1, b_s2 = bank[0], bank[1:3], bank[3], bank[4:6], bank[6:8]

        s = {n: sem(n) for n in (
            "consts_in", "qkv_w_in", "o_w_in", "x_in", "router_in", "xT_in0", "xT_in1",
            "const_ready", "qk_const_ready", "presets", "presets_v", "w_qkv_ready", "w_qkv_hi_ready", "w_o_hi_ready", "w_o_ready",
            "xT_hi_ready", "xT_ready", "qkv_done", "rope_terms", "rope_sum", "qk_hi_ready", "qk_lo_ready",
            "qk_dup_ready", "v_psum_read", "v_ready", "q_transposed", "k_transposed", "q_t_ready", "k_t_ready",
            "k_lead_ready", "s1_done", "max_done", "max_hi_ready", "max_rows_ready", "max_transposed",
            "q_max_ready", "s2_done", "exp_done", "pv_done", "o_tok_ready", "o_inv_ready", "o_norm_ready",
            "o_hi_ready", "o_parts_ready", "o_back_ready", "o_t_ready", "attn_done", "resid_ready", "stats_ready",
            "mean_var_ready", "rstd_step", "z_ready", "z_transposed", "zT_own_ready", "zT_hi_ready",
            "zT_lo_ready", "logits_done", "logits_ready")}

        shared.close()

        def sb(name, shape, dt=F32):
            return ctx.enter_context(nc.sbuf_tensor(name, shape, dt))

        scores_e = sb("scores_e", [P, TILES, E])
        top_val = sb("top_val", [P, TILES, 8])
        top_idx = sb("top_idx", [P, TILES, 8], U32)
        top_idx_f = sb("top_idx_f", [P, TILES, 8])
        top_rel = sb("top_rel", [P, TILES, TOPK])
        top_exp = sb("top_exp", [P, TILES, TOPK])
        top_sum = sb("top_sum", [P, TILES])
        top_inv = sb("top_inv", [P, TILES])
        top_w = sb("top_w", [P, TILES, TOPK])
        top_hot = sb("top_hot", [P, TILES, TOPK, E])
        top_hot_w = sb("top_hot_w", [P, TILES, TOPK, E])
        scores_t = sb("scores_t", [E, T])
        gate = [sb(f"gate{i}", [P, 512]) for i in range(2)]
        up = [sb(f"up{i}", [P, 512]) for i in range(2)]
        up1 = [sb(f"up1_{i}", [P, 512]) for i in range(2)]
        glu = [sb(f"glu{i}", [P, 512]) for i in range(2)]
        hid = [sb(f"hid{i}", [P, 512]) for i in range(2)]
        hid_hi = [sb(f"hid_hi{i}", [P, CC, 512], F32R) for i in range(2)]
        hid_lo = [sb(f"hid_lo{i}", [P, CC, 512], F32R) for i in range(2)]
        acc = sb("acc", [P, TILES, C])
        out_stats = sb("out_stats", [P, TILES, 6])
        out_mv = sb("out_mv", [P, TILES, 2])
        out_var = sb("out_var", [P, TILES])
        out_rstd = sb("out_rstd", [P, TILES])
        for n in ("bias_in", "w_in0", "w_in1", "w_up_hi_ready", "w_dn_hi_ready", "w_up_ready", "w_ready", "gu_free", "gu_done", "gate_ready", "up_ready",
                  "up1_ready", "glu_ready", "hid_ready", "hid_hi_ready", "hid_lo_ready", "hid_free", "y_done", "y_free",
                  "top_done", "top_rel_ready", "top_exp_ready", "top_sum_ready", "top_inv_ready", "top_w_ready",
                  "top_idx_f_ready", "hot_ready", "hot_w_ready", "scores_ready", "scores_transposed", "scores_t_ready",
                  "bias_done", "acc_ready", "out_stats_ready", "out_mv_ready", "out_var_ready", "out_rstd_ready", "out_ready", "stored"):
            s[n] = sem(n)

        def experts(eng, expert):
            expert(0, 0, 0, first=True)
            with eng.Fori(0, E // 2 - 1) as i:
                expert(2 * i + 1, i, 1)
                expert(2 * i + 2, i + 1, 0)
            expert(E - 1, E // 2 - 1, 1, last=True)

        def ffn_sync(sp):
            sp.dma_start(down_b[:, :], a["down_b"]).then_inc(s["bias_in"], 16)
            sp.dma_start(up_b[:, :, :], a["up_b"]).then_inc(s["bias_in"], 16)

            def load(e, k):
                sp.dma_start(w_up[k][:, :, :], a["w_up"].rearrange("e (c p) n -> p e c n", p=P)[:, bass.ds(e, 1), :, :]
                             .rearrange("p o c n -> p (o c) n")).then_inc(s[f"w_in{k}"], 16)
                sp.dma_start(w_dn[k][:, :, :], a["w_dn"].rearrange("e (c p) n -> p e c n", p=P)[:, bass.ds(e, 1), :, :]
                             .rearrange("p o c n -> p (o c) n")).then_inc(s[f"w_in{k}"], 16)

            load(0, 0)
            load(1, 1)
            with sp.Fori(1, E // 2) as i:
                for k in range(2):
                    sp.wait_ge(s["w_ready"], 2 * i + k - 1)
                    load(2 * i + k, k)
            out_t = out.rearrange("b (t p) c -> p (b t) c", p=P)
            for c in range(2):
                sp.wait_ge(s["out_ready"], 4 * c + 4)
                sp.dma_start(out_t[:, 4 * c:4 * c + 4, :], z_res[:, 4 * c:4 * c + 4, :]).then_inc(s["stored"], 16)
            sp.wait_ge(s["stored"], 32)

        def ffn_tensor(pe):
            def unit(e, k, c, h):
                n = 4 * e + 2 * c + h
                if c == 0 and h == 0:
                    pe.wait_ge(s["w_up_ready"], e + 1)
                pe.wait_ge(s["gu_free"], n + 1)
                for m in range(2):
                    w0 = m * D + h * P
                    i = 0
                    for kc in range(CC):
                        for w, z in ((w_up_hi, zT_hi), (w_up_lo, zT_hi), (w_up_hi, zT_lo)):
                            mm = pe.matmul(bank[2 * h + m][:, :], w[k][:, kc, w0:w0 + P], z[:, kc, c * 512:(c + 1) * 512],
                                           start=i == 0, stop=i == 3 * CC - 1)
                            i += 1
                mm.then_inc(s["gu_done"], 1)

            def down(e, k, c):
                if c == 0:
                    pe.wait_ge(s["w_ready"], e + 1)
                pe.wait_ge(s["hid_lo_ready"], 4 * e + 2 * c + 2)
                for pair in range(2):
                    pe.wait_ge(s["y_free"], 4 * e + 2 * c + pair + 1)
                    for tile in range(2):
                        t0 = (2 * pair + tile) * P
                        i = 0
                        for h in range(CC):
                            for x, w in ((hid_hi, w_dn_hi), (hid_lo, w_dn_hi), (hid_hi, w_dn_lo)):
                                mm = pe.matmul(bank[4 + 2 * c + pair][:, tile * C:(tile + 1) * C], x[c][:, h, t0:t0 + P],
                                               w[k][:, h, :], start=i == 0, stop=i == 3 * CC - 1)
                                i += 1
                    mm.then_inc(s["y_done"], 1)

            def score_bias():
                pe.wait_ge(s["scores_ready"], 1)
                pe.wait_ge(s["bias_in"], 32)
                for t in range(TILES):
                    m = pe.transpose(bank[4 + t // 4][0:E, t % 4 * P:(t % 4 + 1) * P], scores_e[:, t, :], ident[:, :])
                m.then_inc(s["scores_transposed"], 1)
                pe.wait_ge(s["scores_t_ready"], 1)
                for b in (6, 7, 4, 5):
                    for tile in range(2):
                        t = 2 * ((b - 6) % 4) + tile
                        m = pe.matmul(bank[b][:, tile * C:(tile + 1) * C], scores_t[:, t * P:(t + 1) * P], down_b[:, :],
                                      start=True, stop=True)
                    m.then_inc(s["bias_done"], 1)

            def expert(e, i, k, first=False, last=False):
                unit(e, k, 0, 0)
                unit(e, k, 0, 1)
                if first:
                    score_bias()
                else:
                    down(e - 1, 1 - k, 1)
                unit(e, k, 1, 0)
                unit(e, k, 1, 1)
                down(e, k, 0)

            pe.wait_ge(s["zT_lo_ready"], TILES)
            experts(pe, expert)
            down(E - 1, 1, 1)

        def ffn_scalar(act):
            def gelu(e, c, h, first):
                n = 4 * e + 2 * c + h
                act.wait_ge(s["gate_ready"], n + 1)
                if not (first and c == 0):
                    act.wait_ge(s["hid_ready"], n - 1)
                act.activation(glu[h][:, :], gate[h][:, :], ACT.Gelu_apprx_sigmoid).then_inc(s["glu_ready"], 1)

            def hi_of_hidden(e, c, h):
                n = 4 * e + 2 * c + h
                act.wait_ge(s["hid_ready"], n + 1)
                if not (isinstance(e, int) and e == 0):
                    act.wait_ge(s["y_done"], 4 * (e - 1) + 2 * c + 2)
                act.activation(hid_hi[c][:, h, :], hid[h][:, :], ACT.Copy).then_inc(s["hid_hi_ready"], 1)

            def split_up(e, i, k, early=False):
                act.wait_ge(s[f"w_in{k}"], 32 * i + 32)
                if not early:
                    act.wait_ge(s["gu_done"], 4 * (e - 1))
                act.activation(w_up_hi[k][:, :, :], w_up[k][:, :, :], ACT.Copy).then_inc(s["w_up_hi_ready"], 1)

            def split_down(e, k, early=False):
                if not early:
                    act.wait_ge(s["y_done"], 4 * (e - 1))
                act.activation(w_dn_hi[k][:, :, :], w_dn[k][:, :, :], ACT.Copy).then_inc(s["w_dn_hi_ready"], 1)

            def expert(e, i, k, first=False, last=False):
                for c in range(2):
                    for h in range(2):
                        gelu(e, c, h, first)
                        hi_of_hidden(e, c, h)
                        if not last and (c, h) == (0, 0):
                            split_up(e + 1, i + k, 1 - k, first)
                        if not last and (c, h) == (0, 1):
                            split_down(e + 1, 1 - k, first)

            split_up(0, 0, 0, True)
            split_down(0, 0, True)
            act.wait_ge(s["top_rel_ready"], 1)
            act.activation(top_exp[:, :, :], top_rel[:, :, :], ACT.Exp).then_inc(s["top_exp_ready"], 1)
            act.wait_ge(s["scores_transposed"], 1)
            for h in range(2):
                m = act.activation(scores_t[:, h * 512:(h + 1) * 512], bank[4 + h][0:E, :], ACT.Copy)
            m.then_inc(s["scores_t_ready"], 1)
            experts(act, expert)

        def ffn_vector(dve):
            def route_weights():
                dve.wait_ge(s["logits_ready"], TILES)
                for t in range(TILES):
                    dve.max(top_val[:, t, :], logits[:, t, :]).then_inc(s["top_done"], 1)
                dve.wait_ge(s["top_done"], TILES)
                for t in range(TILES):
                    dve.max_index(top_idx[:, t, :], top_val[:, t, :], logits[:, t, :]).then_inc(s["top_done"], 1)
                dve.tensor_tensor(top_rel[:, :, :], top_val[:, :, 0:TOPK],
                                  top_val[:, :, 0:1].broadcast_to([P, TILES, TOPK]), ALU.subtract).then_inc(s["top_rel_ready"], 1)
                dve.wait_ge(s["top_done"], 2 * TILES)
                dve.tensor_copy(top_idx_f[:, :, :], top_idx[:, :, :]).then_inc(s["top_idx_f_ready"], 1)
                dve.wait_ge(s["top_idx_f_ready"], 1)
                for r in range(TOPK):
                    m = dve.tensor_tensor(top_hot[:, :, r, :],
                                          expert_no.rearrange("p (o e) -> p o e", o=1).broadcast_to([P, TILES, E]),
                                          top_idx_f[:, :, r:r + 1].broadcast_to([P, TILES, E]), ALU.is_equal)
                m.then_inc(s["hot_ready"], 1)
                dve.wait_ge(s["top_exp_ready"], 1)
                dve.tensor_reduce(top_sum[:, :], top_exp[:, :, :], AX.X, ALU.add).then_inc(s["top_sum_ready"], 1)
                dve.wait_ge(s["top_sum_ready"], 1)
                dve.reciprocal(top_inv[:, :], top_sum[:, :]).then_inc(s["top_inv_ready"], 1)
                dve.wait_ge(s["top_inv_ready"], 1)
                dve.tensor_tensor(top_w[:, :, :], top_exp[:, :, :],
                                  top_inv[:, :].rearrange("p (t o) -> p t o", o=1).broadcast_to([P, TILES, TOPK]), ALU.mult
                                  ).then_inc(s["top_w_ready"], 1)
                dve.wait_ge(s["top_w_ready"], 1)
                dve.wait_ge(s["hot_ready"], 1)
                for r in range(TOPK):
                    m = dve.tensor_tensor(top_hot_w[:, :, r, :], top_hot[:, :, r, :],
                                          top_w[:, :, r:r + 1].broadcast_to([P, TILES, E]), ALU.mult)
                m.then_inc(s["hot_w_ready"], 1)
                dve.wait_ge(s["hot_w_ready"], 1)
                dve.tensor_reduce(scores_e[:, :, :], top_hot_w[:, :, :, :].rearrange("p t r e -> p t e r"), AX.X, ALU.add
                                  ).then_inc(s["scores_ready"], 1)

            def start_acc():
                dve.wait_ge(s["z_ready"], TILES)
                for i, b in enumerate((6, 7, 4, 5)):
                    dve.wait_ge(s["bias_done"], i + 1)
                    t = 2 * ((b - 6) % 4)
                    dve.tensor_tensor(acc[:, t:t + 2, :], bank[b][:, :].rearrange("p (t c) -> p t c", t=2), z_res[:, t:t + 2, :],
                                      ALU.add).then_inc(s["acc_ready"], 1)
                dve.wait_ge(s["acc_ready"], 4)
                dve.sem_inc(s["y_free"], 4)

            def gate_up(e, c, h, first):
                n = 4 * e + 2 * c + h
                dve.wait_ge(s["gu_done"], n + 1)
                if not (first and c == 0):
                    dve.wait_ge(s["glu_ready"], n - 1)
                dve.tensor_scalar(gate[h][:, :], bank[2 * h][:, :], up_b[:, bass.ds(e, 1), h:h + 1].rearrange("p o b -> p (o b)"),
                                  LIMIT, ALU.add, ALU.min).then_inc(s["gate_ready"], 1)
                dve.tensor_scalar(up[h][:, :], bank[2 * h + 1][:, :], up_b[:, bass.ds(e, 1), 2 + h:3 + h].rearrange("p o b -> p (o b)"),
                                  LIMIT, ALU.add, ALU.min).then_inc(s["gu_free"], 1)
                dve.wait_ge(s["gu_free"], n + 3)
                dve.tensor_scalar(up1[h][:, :], up[h][:, :], -LIMIT, 1.0, ALU.max, ALU.add).then_inc(s["up1_ready"], 1)

            def hidden(e, c, h, first=False):
                n = 4 * e + 2 * c + h
                dve.wait_ge(s["glu_ready"], n + 1)
                dve.wait_ge(s["up1_ready"], n + 1)
                if not (first and c == 0):
                    dve.wait_ge(s["hid_lo_ready"], n - 1)
                dve.tensor_tensor(hid[h][:, :], up1[h][:, :], glu[h][:, :], ALU.mult).then_inc(s["hid_ready"], 1)

            def accumulate(e, c):
                for pair in range(2):
                    m = 4 * e + 2 * c + pair
                    dve.wait_ge(s["y_done"], m + 1)
                    dve.wait_ge(s["acc_ready"], m + 1)
                    for tile in range(2):
                        t = 4 * c + 2 * pair + tile
                        i = dve.scalar_tensor_tensor(acc[:, t, :], bank[4 + 2 * c + pair][:, tile * C:(tile + 1) * C],
                                                     scores_e[:, t, bass.ds(e, 1)], acc[:, t, :], ALU.mult, ALU.add)
                    i.then_inc(s["acc_ready"], 1)
                    dve.wait_ge(s["acc_ready"], m + 5)
                    dve.sem_inc(s["y_free"], 1)

            def expert(e, i, k, first=False, last=False):
                for c in range(2):
                    for h in range(2):
                        gate_up(e, c, h, first)
                        hidden(e, c, h, first)
                        if h == 0 and not first:
                            accumulate(e - 1, c)
                        if first and (c, h) == (0, 1):
                            start_acc()

            def finish(c):
                t0 = 4 * c
                for t in range(t0, t0 + 4):
                    dve.bn_stats(out_stats[:, t, :], acc[:, t, :]).then_inc(s["out_stats_ready"], 1)
                dve.wait_ge(s["out_stats_ready"], t0 + 4)
                for t in range(t0, t0 + 4):
                    dve.bn_aggr(out_mv[:, t, :], out_stats[:, t, :]).then_inc(s["out_mv_ready"], 1)

            def apply(c):
                dve.wait_ge(s["out_rstd_ready"], c + 1)
                for t in range(4 * c, 4 * c + 4):
                    dve.tensor_scalar(z_res[:, t, :], acc[:, t, :], out_mv[:, t, 0:1], out_rstd[:, t:t + 1],
                                      ALU.subtract, ALU.mult).then_inc(s["out_ready"], 1)

            dve.sem_inc(s["gu_free"], 2)
            route_weights()
            experts(dve, expert)
            accumulate(E - 1, 0)
            finish(0)
            accumulate(E - 1, 1)
            finish(1)
            apply(0)
            apply(1)

        def ffn_gpsimd(pool):
            def lo_of_hidden(e, c, h):
                n = 4 * e + 2 * c + h
                pool.wait_ge(s["hid_hi_ready"], n + 1)
                pool.tensor_tensor(hid_lo[c][:, h, :], hid[h][:, :], hid_hi[c][:, h, :].bitcast(F32), ALU.subtract
                                   ).then_inc(s["hid_lo_ready"], 1)

            def split_up(e, k):
                pool.wait_ge(s["w_up_hi_ready"], e + 1)
                pool.tensor_tensor(w_up_lo[k][:, :, :], w_up[k][:, :, :], w_up_hi[k][:, :, :].bitcast(F32), ALU.subtract
                                   ).then_inc(s["w_up_ready"], 1)

            def split_down(e, k):
                pool.wait_ge(s["w_dn_hi_ready"], e + 1)
                pool.tensor_tensor(w_dn_lo[k][:, :, :], w_dn[k][:, :, :], w_dn_hi[k][:, :, :].bitcast(F32), ALU.subtract
                                   ).then_inc(s["w_ready"], 1)

            def expert(e, i, k, first=False, last=False):
                for c in range(2):
                    for h in range(2):
                        lo_of_hidden(e, c, h)
                        if not last and (c, h) == (0, 0):
                            split_up(e + 1, 1 - k)
                        if not last and (c, h) == (0, 1):
                            split_down(e + 1, 1 - k)

            def roots(c):
                t = slice(4 * c, 4 * c + 4)
                pool.wait_ge(s["out_mv_ready"], 4 * c + 4)
                pool.tensor_tensor(out_var[:, t], out_mv[:, t, 1], c_eps.broadcast_to([P, 4]), ALU.add
                                   ).then_inc(s["out_var_ready"], 1)
                pool.wait_ge(s["out_var_ready"], c + 1)
                pool.tensor_tensor(out_rstd[:, t], out_var[:, t], c_minus_half.broadcast_to([P, 4]), ALU.pow
                                   ).then_inc(s["out_rstd_ready"], 1)

            split_up(0, 0)
            split_down(0, 0)
            experts(pool, expert)
            roots(0)
            roots(1)

        block = ctx.enter_context(nc.Block())

        def iterations(eng, head, iteration):
            head()
            iteration(0, 0, 0, has_route=False)
            with eng.Fori(0, TILES // 2 - 1) as i:
                iteration(2 * i + 1, i, 1)
                iteration(2 * i + 2, i + 1, 0)
            iteration(TILES - 1, TILES // 2 - 1, 1, has_front=False)

        @block.sync
        def _(sp):
            def load_tile(t, p):
                sp.dma_start(xT[p][:, :, :], a["x_t"].rearrange("(c p) (t n) -> p t c n", p=P, n=P)[:, t, :, :]
                             ).then_inc(s[f"xT_in{p}"], 16)

            load_tile(0, 0)
            sp.dma_start(w_qkv[:, :, :], a["w_qkv"].rearrange("(c p) n -> p c n", p=P)).then_inc(s["qkv_w_in"], 16)
            sp.dma_start(rope[:, :, :], a["c_rope"]).then_inc(s["consts_in"], 16)
            sp.dma_start(small[:, :], a["c_small"]).then_inc(s["consts_in"], 16)
            sp.dma_start(qk_const[:, :, :], a["c_qk"]).then_inc(s["consts_in"], 16)
            load_tile(1, 1)
            sp.dma_start(ident[:, :], a["c_ident"]).then_inc(s["consts_in"], 16)
            sp.dma_start(mask_f[:, :, :], a["c_mask"].rearrange("m p n -> p m n")).then_inc(s["consts_in"], 16)
            sp.dma_start(w_o[:, :, :], a["w_o"].rearrange("(j p) n -> p j n", p=P)).then_inc(s["o_w_in"], 16)
            sp.dma_start(x_res[:, :, :], a["x"].rearrange("(t p) c -> p t c", p=P)).then_inc(s["x_in"], 16)
            sp.dma_start(router[:, :, :], a["router_t"].rearrange("(c p) e -> p c e", p=P)).then_inc(s["router_in"], 16)
            sp.dma_start(router_b[:, :], a["router_b"]).then_inc(s["router_in"], 16)
            with sp.Fori(1, TILES // 2) as i:
                for p in range(2):
                    sp.wait_ge(s["xT_ready"], 2 * i + p - 1)
                    load_tile(2 * i + p, p)
            ffn_sync(sp)

        @block.tensor
        def _(pe):
            def qkv(t, p):
                pe.wait_ge(s["xT_ready"], t + 1)
                n = 0
                for c in range(CC):
                    for x, w in ((xT_hi, w_qkv_hi), (xT_lo, w_qkv_hi), (xT_hi, w_qkv_lo)):
                        m = pe.matmul(b_mix[:, 0:QKV], x[p][:, c, :], w[:, c, :], start=n == 0, stop=n == 3 * CC - 1)
                        n += 1
                m.then_inc(s["qkv_done"], 1)

            def transpose_qk(t, p):
                pe.wait_ge(s["qk_lo_ready"], t + 1)
                pe.wait_ge(s["qk_dup_ready"], t + 1)
                for h in range(HALVES):
                    for j in range(REP):
                        f = (h * REP + j) * GRP
                        m = pe.transpose(b_qt[h][:, j * P:(j + 1) * P], qk_parts[p][:, f:f + GRP, :].bitcast(F32), ident[:, :])
                    m.then_inc(s["q_transposed"], 1)
                pe.wait_ge(s["v_psum_read"], t + 1)
                for h in range(HALVES):
                    f = HEADS + h * GRP
                    m = pe.transpose(b_mix[:, h * P:(h + 1) * P], qk_parts[p][:, f:f + GRP, :].bitcast(F32), ident[:, :])
                m.then_inc(s["k_transposed"], 1)

            def scores_for_max(t, p, n, early):
                h, qt, pp = n // 4, n // 2 % 2, n % 2
                if n == 0:
                    pe.wait_ge(s["q_t_ready"], 2 * t + 2)
                    pe.wait_ge(s["k_t_ready"], t + 1)
                    pe.wait_ge(s["k_lead_ready"], t + 1)
                if not (early and n < 2):
                    pe.wait_ge(s["max_done"], 8 * t + n - 1)
                b = b_s1[n % 2]
                pe.matmul(b[:, :], ident_b[:, :], mask[:, 0, :], start=True, stop=False)
                j = h * REP + 2 * pp
                pe.matmul(b[:, :], q_t[p][:, qt, j:j + 2, :].rearrange("p j q -> p (j q)"),
                          k_t[p][:, h * GRP:(h + 1) * GRP, qt * Q:qt * Q + P], start=False, stop=True
                          ).then_inc(s["s1_done"], 1)

            def transpose_max(t, h):
                pe.wait_ge(s["max_rows_ready"], 2 * t + h + 1)
                for block in range(4):
                    m = pe.transpose(b_qt[h][:, block * P:(block + 1) * P], max_rows[:, 4 * h + block, :, :].bitcast(F32),
                                     ident[:, :])
                m.then_inc(s["max_transposed"], 1)

            def scores(t, p, n, early):
                h, qt, gp = n // 4, n // 2 % 2, n % 2
                if n % 4 == 0:
                    pe.wait_ge(s["q_max_ready"], 2 * t + h + 1)
                if not (early and n < 2):
                    pe.wait_ge(s["exp_done"], 8 * t + n - 1)
                b = b_s2[n % 2]
                pe.matmul(b[:, :], ident_b[:, :], mask[:, 1, :], start=True, stop=False)
                for g in range(2):
                    m = pe.matmul(b[:, g * 256:(g + 1) * 256], k_t[p][:, h * GRP + 2 * gp + g, qt * Q:qt * Q + P],
                                  q_max[p][:, qt, h * REP:(h + 1) * REP, :], start=False, stop=g == 1)
                m.then_inc(s["s2_done"], 1)

            def values(t, p, n, early):
                h, qt, gp = n // 4, n // 2 % 2, n % 2
                if n == 0:
                    pe.wait_ge(s["v_ready"], t + 1)
                if n % 4 == 0 and not (early and n == 0):
                    pe.wait_ge(s["o_tok_ready"], 2 * t + h)
                pe.wait_ge(s["exp_done"], 8 * t + n + 1)
                v = (v_lead, v_own)[qt][p]
                for g in range(2):
                    r = (2 * gp + g) * FEAT
                    m = pe.matmul(b_o[r:r + FEAT, qt * 256:(qt + 1) * 256], v[:, h * GRP + 2 * gp + g, :],
                                  probs[n % 4][:, g * 256:(g + 1) * 256], start=True, stop=True)
                m.then_inc(s["pv_done"], 1)

            def out_proj(t):
                pe.wait_ge(s["o_t_ready"], 2 * t + 2)
                for j in range(HALVES * REP):
                    m = pe.matmul(b_mix[:, 0:C], o_t[:, j, :], w_o3[:, j, :], start=j == 0, stop=j == HALVES * REP - 1)
                m.then_inc(s["attn_done"], 1)

            def transpose_z(t, p):
                pe.wait_ge(s["z_ready"], t + 1)
                for c in range(CC):
                    m = pe.transpose(b_qt[1][:, c * P:(c + 1) * P], z_tile[p][:, c * P:(c + 1) * P], ident[:, :])
                m.then_inc(s["z_transposed"], 1)

            def route(t):
                pe.wait_ge(s["zT_hi_ready"], t + 1)
                for c in range(CC):
                    pe.matmul(b_qt[1][:, 0:E], zT_own[:, c, :], router[:, c, :], start=c == 0, stop=False)
                pe.matmul(b_qt[1][:, 0:E], ones_row[:, :], router_b[:, :], start=False, stop=True
                          ).then_inc(s["logits_done"], 1)

            def head():
                pe.wait_ge(s["w_qkv_ready"], 1)
                qkv(0, 0)
                pe.wait_ge(s["const_ready"], 1)
                transpose_qk(0, 0)
                for n in range(8):
                    scores_for_max(0, 0, n, True)
                    if n == 4:
                        transpose_max(0, 0)
                transpose_max(0, 1)
                pe.wait_ge(s["w_o_ready"], 1)
                pe.wait_ge(s["router_in"], 32)

            def iteration(t, half_t, p, has_route=True, has_front=True):
                early = not has_route
                scores(t, p, 0, early)
                scores(t, p, 1, early)
                if has_front:
                    if has_route:
                        pe.wait_ge(s["resid_ready"], t)
                    else:
                        pe.wait_ge(s["k_t_ready"], 1)
                    qkv(t + 1, 1 - p)
                for n in range(3):
                    values(t, p, n, early)
                    scores(t, p, n + 2, early)
                values(t, p, 3, early)
                scores(t, p, 5, early)
                if has_front:
                    transpose_qk(t + 1, 1 - p)
                for n in range(4, 8):
                    values(t, p, n, early)
                    if n + 2 < 8:
                        scores(t, p, n + 2, early)
                    if has_front:
                        scores_for_max(t + 1, 1 - p, n - 4, False)
                if has_route:
                    transpose_z(t - 1, 1 - p)
                if has_front:
                    for n in range(4, 8):
                        scores_for_max(t + 1, 1 - p, n, False)
                        if n == 4:
                            transpose_max(t + 1, 0)
                        if n == 5 and has_route:
                            route(t - 1)
                elif has_route:
                    route(t - 1)
                if has_front:
                    pe.wait_ge(s["k_t_ready"], t + 2)
                else:
                    pe.wait_ge(s["resid_ready"], t)
                out_proj(t)
                if has_front:
                    if has_route:
                        pe.wait_ge(s["logits_ready"], t)
                    transpose_max(t + 1, 1)

            iterations(pe, head, iteration)
            pe.wait_ge(s["resid_ready"], TILES)
            transpose_z(TILES - 1, 1)
            route(TILES - 1)
            pe.wait_ge(s["logits_ready"], TILES)
            ffn_tensor(pe)

        @block.scalar
        def _(act):
            def v_copies(t, p, early):
                act.wait_ge(s["rope_terms"], t + 1)
                if not early:
                    act.wait_ge(s["pv_done"], 8 * (t - 1))
                v = b_mix[:, C + KV * DH:QKV].rearrange("p (k d) -> p k d", d=DH)
                act.activation(v_own[p][:, :, 0:DH], v, ACT.Copy)
                act.activation(v_lead[p][Q:P, :, 0:DH], v[0:Q], ACT.Copy).then_inc(s["v_psum_read"], 1)

            def q_copies(t, p):
                for h in range(HALVES):
                    act.wait_ge(s["q_transposed"], 2 * t + h + 1)
                    act.activation(q_t[p][:, :, h * REP:(h + 1) * REP, :],
                                   b_qt[h][:, :].rearrange("p (j s q) -> p s j q", j=REP, s=2), ACT.Copy
                                   ).then_inc(s["q_t_ready"], 1)

            def exponentials(t, n, early):
                act.wait_ge(s["s2_done"], 8 * t + n + 1)
                if not (early and n < 4):
                    act.wait_ge(s["pv_done"], 8 * t + n - 3)
                act.activation(probs[n % 4][:, :], b_s2[n % 2][:, :], ACT.Exp, scale=float(DH) ** -0.5
                               ).then_inc(s["exp_done"], 1)

            def normalised(t, p):
                act.wait_ge(s["rstd_step"], ROOT_STEPS * t + ROOT_STEPS)
                act.activation(z_tile[p][:, :], resid[:, :], ACT.Identity, bias=shift[:, :], scale=rstd[:, :])
                act.activation(z_res[:, bass.ds(t, 1), :].rearrange("p o c -> p (o c)"), resid[:, :], ACT.Identity,
                               bias=shift[:, :], scale=rstd[:, :]).then_inc(s["z_ready"], 1)

            def o_copy(t, h, early):
                act.wait_ge(s["o_back_ready"], 2 * t + h + 1)
                if not early and h == 0:
                    act.wait_ge(s["attn_done"], t)
                act.activation(o_t[:, h * REP:(h + 1) * REP, :].rearrange("p j (s q) -> p j s q", s=2),
                               o_back[h][:, :].rearrange("p (s j q) -> p j s q", s=2, j=REP), ACT.Copy
                               ).then_inc(s["o_t_ready"], 1)

            def z_copies(t):
                act.wait_ge(s["z_transposed"], t + 1)
                zp = b_qt[1][:, 0:C].rearrange("p (c n) -> p c n", c=CC)
                act.activation(zT_own[:, :, :], zp, ACT.Copy).then_inc(s["zT_own_ready"], 1)
                act.activation(zT_hi[:, :, bass.ts(t, P)], zp, ACT.Copy).then_inc(s["zT_hi_ready"], 1)

            def logits_copy(t):
                act.wait_ge(s["logits_done"], t + 1)
                act.activation(logits[:, bass.ds(t, 1), :], b_qt[1][:, 0:E].rearrange("p (o e) -> p o e", o=1), ACT.Copy
                               ).then_inc(s["logits_ready"], 1)

            def front_v(t, p, first, early):
                v_copies(t, p, early)
                if not first:
                    act.wait_ge(s["v_psum_read"], t + 1)
                act.activation(v_lead[p][0:Q, :, 0:DH], (v_own[1 - p] if not first else v_zero)[Q:P, :, 0:DH], ACT.Copy
                               ).then_inc(s["v_ready"], 1)

            v_zero = v_own[1]

            def head():
                act.wait_ge(s["presets_v"], 1)
                front_v(0, 0, True, True)
                q_copies(0, 0)

            def iteration(t, half_t, p, has_route=True, has_front=True):
                early = not has_route
                for n in range(3):
                    exponentials(t, n, early)
                if has_front:
                    front_v(t + 1, 1 - p, False, early)
                exponentials(t, 3, early)
                exponentials(t, 4, early)
                if has_route:
                    normalised(t - 1, 1 - p)
                if has_front:
                    q_copies(t + 1, 1 - p)
                exponentials(t, 5, early)
                exponentials(t, 6, early)
                o_copy(t, 0, early)
                exponentials(t, 7, early)
                if has_route:
                    z_copies(t - 1)
                    logits_copy(t - 1)
                o_copy(t, 1, early)

            iterations(act, head, iteration)
            normalised(TILES - 1, 1)
            z_copies(TILES - 1)
            logits_copy(TILES - 1)
            ffn_scalar(act)

        @block.vector
        def _(dve):
            def rope_qk(t, p, early):
                dve.wait_ge(s["qkv_done"], t + 1)
                qk = b_mix[:, 0:QK_HEADS * DH].rearrange("p (h d) -> p h d", d=DH)
                hd = DH // 2
                tab = rope[:, bass.ds(t, 1), :]

                def table(lo, n):
                    return tab[:, :, lo:lo + n].broadcast_to([P, QK_HEADS, n])

                if not early:
                    dve.wait_ge(s["qk_dup_ready"], t)
                dve.tensor_tensor(rope_a[:, :, :], qk, table(0, DH), ALU.mult)
                dve.tensor_tensor(rope_b[:, :, 0:hd], qk[:, :, hd:DH], table(DH, hd), ALU.mult)
                dve.tensor_tensor(rope_b[:, :, hd:DH], qk[:, :, 0:hd], table(DH + hd, hd), ALU.mult
                                  ).then_inc(s["rope_terms"], 1)
                dve.wait_ge(s["rope_terms"], t + 1)
                dve.tensor_tensor(roped[:, :, :], rope_a[:, :, :], rope_b[:, :, :], ALU.add).then_inc(s["rope_sum"], 1)
                dve.wait_ge(s["rope_sum"], t + 1)
                if not early:
                    dve.wait_ge(s["k_transposed"], t - 1)
                parts = qk_parts[p]
                dve.tensor_copy(parts[:, :, 0:DH], roped[:, :, :]).then_inc(s["qk_hi_ready"], 1)
                dve.wait_ge(s["qk_hi_ready"], t + 1)
                dve.tensor_tensor(parts[:, 0:HEADS, 2 * DH:3 * DH], roped[:, 0:HEADS, :],
                                  parts[:, 0:HEADS, 0:DH].bitcast(F32), ALU.subtract)
                dve.tensor_tensor(parts[:, HEADS:QK_HEADS, DH:2 * DH], roped[:, HEADS:QK_HEADS, :],
                                  parts[:, HEADS:QK_HEADS, 0:DH].bitcast(F32), ALU.subtract).then_inc(s["qk_lo_ready"], 1)

            def k_copies(t, p, early):
                dve.wait_ge(s["k_transposed"], t + 1)
                if not early:
                    dve.wait_ge(s["s2_done"], 8 * (t - 1))
                    dve.wait_ge(s["k_lead_ready"], t)
                for h in range(HALVES):
                    m = dve.tensor_tensor(
                        k_t[p][:, h * GRP:(h + 1) * GRP, WINDOW:WINDOW + P],
                        b_mix[:, h * P:(h + 1) * P].rearrange("p (o n) -> p o n", o=1).broadcast_to([P, GRP, P]),
                        group_of.rearrange("p (g o) -> p g o", o=1).broadcast_to([P, GRP, P]), ALU.mult)
                m.then_inc(s["k_t_ready"], 1)

            def row_max(t, n):
                dve.wait_ge(s["s1_done"], 8 * t + n + 1)
                dve.tensor_reduce(neg_max[:, n, :], b_s1[n % 2][:, :].rearrange("p (g k) -> p g k", g=GRP),
                                  AX.X, ALU.max, negate=True).then_inc(s["max_done"], 1)

            def max_parts(t, h, first):
                dve.wait_ge(s["max_done"], 8 * t + 4 * h + 4)
                if not first:
                    dve.wait_ge(s["max_transposed"], 2 * t + h - 1)
                rows, value = max_rows[:, 4 * h:4 * h + 4], neg_max[:, 4 * h:4 * h + 4, :].rearrange("p n (g o) -> p n g o", o=1)
                dve.tensor_copy(rows[:, :, :, ROW_NEGMAX:ROW_NEGMAX + 1], value).then_inc(s["max_hi_ready"], 1)
                dve.wait_ge(s["max_hi_ready"], 2 * t + h + 1)
                dve.tensor_tensor(rows[:, :, :, ROW_NEGMAX + 1:ROW_NEGMAX + 2], value,
                                  rows[:, :, :, ROW_NEGMAX:ROW_NEGMAX + 1].bitcast(F32), ALU.subtract
                                  ).then_inc(s["max_rows_ready"], 1)

            def add_max(t, p, h, early):
                dve.wait_ge(s["max_transposed"], 2 * t + h + 1)
                if not early and h == 0:
                    dve.wait_ge(s["s2_done"], 8 * (t - 1))
                dve.tensor_tensor(q_max[p][:, :, h * REP:(h + 1) * REP, :],
                                  b_qt[h][:, :].rearrange("p (s j q) -> p s j q", s=2, j=REP),
                                  q_t[p][:, :, h * REP:(h + 1) * REP, :].bitcast(F32), ALU.add
                                  ).then_inc(s["q_max_ready"], 1)

            def take_values(t, h):
                dve.wait_ge(s["pv_done"], 8 * t + 4 * h + 4)
                dve.transpose(o_tok[:, :, :].rearrange("p b f -> p (b f)"), b_o[:, :]).then_inc(s["o_tok_ready"], 1)

            def normalise(t, h, first):
                n = 2 * t + h
                dve.wait_ge(s["o_tok_ready"], n + 1)
                dve.reciprocal(o_inv[:, :], o_tok[:, :, DH]).then_inc(s["o_inv_ready"], 1)
                dve.wait_ge(s["o_inv_ready"], n + 1)
                dve.tensor_tensor(o_norm[:, :, :], o_tok[:, :, 0:DH],
                                  o_inv[:, :].rearrange("p (b o) -> p b o", o=1).broadcast_to([P, 16, DH]), ALU.mult
                                  ).then_inc(s["o_norm_ready"], 1)
                dve.wait_ge(s["o_norm_ready"], n + 1)
                dve.tensor_copy(o_parts[:, :, 0:DH], o_norm[:, :, :]).then_inc(s["o_hi_ready"], 1)
                dve.tensor_copy(o_parts[:, :, 2 * DH:3 * DH], o_norm[:, :, :])
                dve.wait_ge(s["o_hi_ready"], n + 1)
                dve.tensor_tensor(o_parts[:, :, DH:2 * DH], o_norm[:, :, :], o_parts[:, :, 0:DH].bitcast(F32), ALU.subtract
                                  ).then_inc(s["o_parts_ready"], 1)
                dve.wait_ge(s["o_parts_ready"], n + 1)
                if not first:
                    dve.wait_ge(s["o_t_ready"], n - 1)
                dve.transpose(o_back[h][:, :], o_parts[:, :, :].rearrange("p b f -> p (b f)").bitcast(F32)
                              ).then_inc(s["o_back_ready"], 1)

            def residual(t, first):
                dve.wait_ge(s["attn_done"], t + 1)
                if not first:
                    dve.wait_ge(s["z_ready"], t)
                dve.tensor_tensor(resid[:, :], b_mix[:, 0:C], x_res[:, bass.ds(t, 1), :].rearrange("p o c -> p (o c)"), ALU.add
                                  ).then_inc(s["resid_ready"], 1)
                dve.wait_ge(s["resid_ready"], t + 1)
                dve.bn_stats(stats[:, :], resid[:, :]).then_inc(s["stats_ready"], 1)
                wait_apart(dve, s["stats_ready"], t + 1, s["x_in"], 16)
                dve.bn_aggr(mean_var[:, :], stats[:, :]).then_inc(s["mean_var_ready"], 1)

            def setup():
                dve.wait_ge(s["qkv_w_in"], 16)
                dve.tensor_copy(w_qkv_hi[:, :, :], w_qkv[:, :, :]).then_inc(s["w_qkv_hi_ready"], 1)
                dve.wait_ge(s["w_qkv_hi_ready"], 1)
                dve.tensor_tensor(w_qkv_lo[:, :, :], w_qkv[:, :, :], w_qkv_hi[:, :, :].bitcast(F32), ALU.subtract
                                  ).then_inc(s["w_qkv_ready"], 1)
                dve.wait_ge(s["consts_in"], 80)
                dve.tensor_copy(ident_b[:, :], ident[:, :])
                dve.tensor_copy(mask[:, :, :], mask_f[:, :, :]).then_inc(s["const_ready"], 1)
                dve.wait_ge(s["presets"], 1)

            def setup_late():
                dve.wait_ge(s["o_w_in"], 16)
                dve.tensor_copy(w_o_hi[:, :, :], w_o[:, :, :]).then_inc(s["w_o_hi_ready"], 1)
                dve.wait_ge(s["w_o_hi_ready"], 1)
                dve.scalar_tensor_tensor(w_o3[:, :, :], w_o_hi[:, :, :].bitcast(F32), lo_row, w_o[:, :, :],
                                         ALU.mult, ALU.add).then_inc(s["w_o_ready"], 1)
                dve.wait_ge(s["x_in"], 16)

            def head():
                setup()
                rope_qk(0, 0, True)
                setup_late()
                k_copies(0, 0, True)
                for n in range(8):
                    row_max(0, n)
                    if n == 3:
                        max_parts(0, 0, True)
                    if n == 5:
                        add_max(0, 0, 0, True)
                max_parts(0, 1, True)
                add_max(0, 0, 1, True)

            def iteration(t, half_t, p, has_route=True, has_front=True):
                first = not has_route
                if has_front:
                    rope_qk(t + 1, 1 - p, first)
                take_values(t, 0)
                if has_front:
                    k_copies(t + 1, 1 - p, first)
                normalise(t, 0, first)
                if has_front:
                    for n in range(4):
                        row_max(t + 1, n)
                    max_parts(t + 1, 0, False)
                take_values(t, 1)
                normalise(t, 1, first)
                if has_front:
                    row_max(t + 1, 4)
                    row_max(t + 1, 5)
                    add_max(t + 1, 1 - p, 0, first)
                    row_max(t + 1, 6)
                    row_max(t + 1, 7)
                    max_parts(t + 1, 1, False)
                residual(t, first)
                if has_front:
                    add_max(t + 1, 1 - p, 1, first)

            iterations(dve, head, iteration)
            ffn_vector(dve)

        @block.gpsimd
        def _(pool):
            def copy(to, from_, shape):
                return pool.tensor_tensor(to, from_, c_one.rearrange("p (a b) -> p a b", a=1).broadcast_to(shape), ALU.mult)

            def split_x(t, half_t, p, early):
                if not early:
                    pool.wait_ge(s["qkv_done"], t - 1)
                pool.wait_ge(s[f"xT_in{p}"], 16 * half_t + 16)
                copy(xT_hi[p][:, :, :], xT[p][:, :, :], [P, CC, P]).then_inc(s["xT_hi_ready"], 1)
                pool.wait_ge(s["xT_hi_ready"], t + 1)
                pool.tensor_tensor(xT_lo[p][:, :, :], xT[p][:, :, :], xT_hi[p][:, :, :].bitcast(F32), ALU.subtract
                                   ).then_inc(s["xT_ready"], 1)

            def duplicate_hi(t, p, early):
                if not early:
                    pool.wait_ge(s["k_transposed"], t - 1)
                pool.wait_ge(s["rope_sum"], t + 1)
                parts = qk_parts[p]
                copy(parts[:, 0:HEADS, DH:2 * DH], roped[:, 0:HEADS, :], [P, HEADS, DH])
                copy(parts[:, HEADS:QK_HEADS, 2 * DH:3 * DH], roped[:, HEADS:QK_HEADS, :], [P, KV, DH]
                     ).then_inc(s["qk_dup_ready"], 1)

            def carry_keys(t, p, early):
                if not early:
                    pool.wait_ge(s["s2_done"], 8 * (t - 1))
                pool.wait_ge(s["k_t_ready"], t)
                copy(k_t[p][:, :, 0:WINDOW], k_t[1 - p][:, :, P:P + WINDOW].bitcast(F32), [P, KV, WINDOW]
                     ).then_inc(s["k_lead_ready"], 1)

            def root(t):
                n = ROOT_STEPS * t

                def step(k, out_, x, y, op):
                    pool.tensor_tensor(out_, x, y, op).then_inc(s["rstd_step"], 1)
                    pool.wait_ge(s["rstd_step"], n + k)

                pool.wait_ge(s["mean_var_ready"], t + 1)
                step(1, var_eps[:, :], mean_var[:, 1:2], c_eps, ALU.add)
                step(2, rstd[:, :], var_eps[:, :], c_minus_half, ALU.pow)
                step(3, mean_rstd[:, :], mean_var[:, 0:1], rstd[:, :], ALU.mult)
                step(4, shift[:, :], mean_rstd[:, :], c_minus_one, ALU.mult)

            def lo_of_z(t):
                pool.wait_ge(s["zT_hi_ready"], t + 1)
                pool.tensor_tensor(zT_lo[:, :, bass.ts(t, P)], zT_own[:, :, :], zT_hi[:, :, bass.ts(t, P)].bitcast(F32),
                                   ALU.subtract).then_inc(s["zT_lo_ready"], 1)

            def head():
                pool.memset(ones_row[:, :], 1.0)
                for c, value in ((c_eps, EPS), (c_minus_half, -0.5), (c_minus_one, -1.0), (c_one, 1.0)):
                    pool.memset(c, value)
                for v in (*v_lead, *v_own):
                    pool.memset(v[:, :, :], 0.0)
                pool.memset(o_parts[:, :, :].bitcast(F32), 0.0)
                pool.memset(max_rows[:, :, :, :].bitcast(F32), 0.0).then_inc(s["presets"], 1)
                pool.wait_ge(s["presets"], 1)
                split_x(0, 0, 0, True)
                for v in (*v_lead, *v_own):
                    m = pool.memset(v[:, :, DH:DH + 1], 1.0)
                m.then_inc(s["presets_v"], 1)
                pool.wait_ge(s["consts_in"], 80)
                for parts in qk_parts:
                    m = pool.tensor_copy(parts[:, :, 3 * DH:FEAT], qk_const[:, :, :])
                m.then_inc(s["qk_const_ready"], 1)
                pool.tensor_copy(k_t[0][:, :, 0:WINDOW],
                                 key_pad.rearrange("p (k o) -> p k o", o=1).broadcast_to([P, KV, WINDOW])
                                 ).then_inc(s["k_lead_ready"], 1)
                duplicate_hi(0, 0, True)

            def iteration(t, half_t, p, has_route=True, has_front=True):
                first = not has_route
                if has_front:
                    split_x(t + 1, half_t + p, 1 - p, first)
                if has_route:
                    root(t - 1)
                if has_front:
                    duplicate_hi(t + 1, 1 - p, first)
                    carry_keys(t + 1, 1 - p, first)
                if has_route:
                    lo_of_z(t - 1)

            iterations(pool, head, iteration)
            root(TILES - 1)
            lo_of_z(TILES - 1)
            ffn_gpsimd(pool)


_INPUTS = ("x", "x_t", "w_qkv", "w_o", "router_t", "router_b", "w_up", "w_dn", "up_b", "down_b",
           "c_rope", "c_ident", "c_mask", "c_small", "c_qk")


def kernel(L0_attn_x, L0_attn_wq, L0_attn_wk, L0_attn_wv, L0_attn_wo, L0_ffn_router_weight, L0_ffn_router_bias,
           L0_ffn_gate_up_proj, L0_ffn_gate_up_proj_bias, L0_ffn_down_proj, L0_ffn_down_proj_bias):
    from concourse import bacc
    from concourse.bass_utils import run_bass_kernel_spmd

    x = np.asarray(L0_attn_x)[0]
    wq = np.asarray(L0_attn_wq).reshape(C, HALVES, GRP, REP, DH).transpose(0, 1, 3, 2, 4).reshape(C, C)
    wo = np.asarray(L0_attn_wo).reshape(HALVES, GRP, REP, DH, C).transpose(0, 2, 1, 3, 4)
    wo3 = np.zeros((HALVES, REP, GRP, FEAT, C), wo.dtype)
    for r in range(3):
        wo3[:, :, :, r * DH:(r + 1) * DH] = wo
    gu = np.asarray(L0_ffn_gate_up_proj).reshape(E, C, D, 2).transpose(0, 1, 3, 2).reshape(E, C, 2 * D)
    gub = np.asarray(L0_ffn_gate_up_proj_bias).reshape(E, CC, P, 2).transpose(2, 0, 3, 1).reshape(P, E, 4)
    arrays = {
        "x": x, "x_t": x.T, "w_qkv": np.concatenate([wq, np.asarray(L0_attn_wk), np.asarray(L0_attn_wv)], 1),
        "w_o": wo3.reshape(HALVES * REP * P, C), "router_t": np.asarray(L0_ffn_router_weight).T,
        "router_b": np.asarray(L0_ffn_router_bias)[None, :], "w_up": gu, "w_dn": np.asarray(L0_ffn_down_proj),
        "up_b": gub, "down_b": np.asarray(L0_ffn_down_proj_bias), **constants(),
    }
    nc = bacc.Bacc("TRN2", target_bir_lowering=False, num_devices=1)
    arrays = {n: np.ascontiguousarray(arrays[n]) for n in _INPUTS}
    aps = {n: nc.dram_tensor("in_" + n, v.shape, mybir.dt.from_np(v.dtype), kind="ExternalInput").ap() for n, v in arrays.items()}
    out = nc.dram_tensor("out", (1, T, C), F32, kind="ExternalOutput").ap()
    build(nc, aps, out)
    r = run_bass_kernel_spmd(nc, [{"in_" + n: v for n, v in arrays.items()}], core_ids=[0])
    return r.results[0]["out"]
```

```python
from contextlib import ExitStack

import numpy as np

import concourse.bass as bass
from concourse import mybir

ALU = mybir.AluOpType
ACT = mybir.ActivationFunctionType
AX = mybir.AxisListType
F32 = mybir.dt.float32
F32R = mybir.dt.float32r
BF16 = mybir.dt.bfloat16
I32 = mybir.dt.int32
U32 = mybir.dt.uint32

T, C = 1024, 256
HEADS, KV, DH = 32, 8, 8
WINDOW = 64
REP = HEADS // KV
P = 128
TILES = T // P
Q = 64
CC = C // P
FEAT = 32
GRP = 4
HALVES = KV // GRP
ROW_NEGMAX = 3 * DH
ROW_PAD = 3 * DH + 2
NEG = -1e30
E, D, TOPK = 16, 256, 4
ALPHA, LIMIT = 1.702, 7.0
EPS = 1e-5
ROOT_STEPS = 4
QKV = C + 2 * KV * DH
QK_HEADS = HEADS + KV


def wait_apart(eng, semaphore, value, settled, settled_value):
    eng.wait_ge(settled, settled_value)
    eng.wait_ge(semaphore, value)


def constants():
    inv = (1.0 / 10000.0 ** (np.arange(0, DH, 2, dtype=np.float32) / np.float32(DH))).astype(np.float32)
    ang = np.arange(T, dtype=np.float32)[:, None] * inv[None, :]
    cos, sin = np.cos(ang).astype(np.float32), np.sin(ang).astype(np.float32)
    rope = np.concatenate([cos, cos, -sin, sin], 1).reshape(TILES, P, 2 * DH).transpose(1, 0, 2)
    ident = np.eye(P, dtype=np.float32)
    qi, ki = np.arange(Q)[:, None], np.arange(P)[None, :]
    ok = (ki <= qi + WINDOW) & (ki >= qi)
    mask = np.where(ok, 0.0, NEG).astype(np.float32)
    mask_q = np.tile(np.concatenate([mask, mask], 0), (1, GRP))
    mask_k = np.tile(mask.T, (1, 8))
    group = np.zeros((P, GRP), np.float32)
    for g in range(GRP):
        group[g * FEAT:(g + 1) * FEAT, g] = 1.0
    key_pad = np.zeros((P, KV), np.float32)
    for k in range(KV):
        key_pad[(k % GRP) * FEAT + ROW_PAD, k] = NEG
    lo_row = np.zeros((P, 1), np.float32)
    for g in range(GRP):
        lo_row[g * FEAT + 2 * DH:g * FEAT + 3 * DH] = -1.0
    small = np.concatenate([group, key_pad, lo_row, np.tile(np.arange(E, dtype=np.float32), (P, 1))], 1)
    qk_const = np.zeros((P, QK_HEADS, DH), np.float32)
    qk_const[:, :HEADS, ROW_PAD - 3 * DH] = 1.0
    qk_const[:, HEADS:, 0:2] = 1.0
    return {"c_rope": np.ascontiguousarray(rope), "c_ident": ident, "c_mask": np.stack([mask_q, mask_k]),
            "c_small": small, "c_qk": qk_const}


def build(nc, a, out):
    with ExitStack() as ctx:
        def sb(name, shape, dt=F32):
            return ctx.enter_context(nc.sbuf_tensor(name, shape, dt))

        def sem(name):
            return ctx.enter_context(nc.semaphore(name))

        rope = sb("rope", [P, TILES, 2 * DH])
        ident = sb("ident", [P, P])
        ident_b = sb("ident_b", [P, P], BF16)
        mask_f = sb("mask_f", [P, 2, 512])
        mask = sb("mask", [P, 2, 512], BF16)
        small = sb("small", [P, GRP + KV + 1 + E])
        group_of = small[:, 0:GRP]
        key_pad = small[:, GRP:GRP + KV]
        lo_row = small[:, GRP + KV:GRP + KV + 1]
        expert_no = small[:, GRP + KV + 1:GRP + KV + 1 + E]
        qk_const = sb("qk_const", [P, QK_HEADS, DH])
        x_res = sb("x_res", [P, TILES, C])
        z_res = sb("z_res", [P, TILES, C])
        zT_hi = sb("zT_hi", [P, CC, T], F32R)
        zT_lo = sb("zT_lo", [P, CC, T], F32R)
        logits = sb("logits", [P, TILES, E])
        router = sb("router", [P, CC, E])
        router_b = sb("router_b", [1, E])
        ones_row = sb("ones_row", [1, P])
        w_qkv = sb("w_qkv", [P, CC, QKV])
        w_qkv_hi = sb("w_qkv_hi", [P, CC, QKV], F32R)
        w_qkv_lo = sb("w_qkv_lo", [P, CC, QKV], F32R)
        w_o = sb("w_o", [P, HALVES * REP, C])
        w_o_hi = sb("w_o_hi", [P, HALVES * REP, C], F32R)
        w_o3 = sb("w_o3", [P, HALVES * REP, C], F32R)
        root_consts = sb("root_consts", [P, 4])
        c_eps, c_minus_half, c_minus_one, c_one = (root_consts[:, i:i + 1] for i in range(4))
        down_b = sb("down_b", [E, C])
        up_b = sb("up_b", [P, E, 4])
        w_up = [sb(f"w_up{i}", [P, CC, 2 * D]) for i in range(2)]
        w_up_hi = [sb(f"w_up_hi{i}", [P, CC, 2 * D], F32R) for i in range(2)]
        w_up_lo = [sb(f"w_up_lo{i}", [P, CC, 2 * D], F32R) for i in range(2)]
        w_dn = [sb(f"w_dn{i}", [P, CC, C]) for i in range(2)]
        w_dn_hi = [sb(f"w_dn_hi{i}", [P, CC, C], F32R) for i in range(2)]
        w_dn_lo = [sb(f"w_dn_lo{i}", [P, CC, C], F32R) for i in range(2)]
        shared = ctx.enter_context(ExitStack())

        def sb(name, shape, dt=F32):
            return shared.enter_context(nc.sbuf_tensor(name, shape, dt))

        xT = [sb(f"xT{p}", [P, CC, P]) for p in range(2)]
        xT_hi = [sb(f"xT_hi{p}", [P, CC, P], F32R) for p in range(2)]
        xT_lo = [sb(f"xT_lo{p}", [P, CC, P], F32R) for p in range(2)]
        qk_parts = [sb(f"qk_parts{p}", [P, QK_HEADS, FEAT], F32R) for p in range(2)]
        q_t = [sb(f"q_t{p}", [P, 2, HALVES * REP, Q], F32R) for p in range(2)]
        q_max = [sb(f"q_max{p}", [P, 2, HALVES * REP, Q], F32R) for p in range(2)]
        k_t = [sb(f"k_t{p}", [P, KV, WINDOW + P], F32R) for p in range(2)]
        v_lead = [sb(f"v_lead{p}", [P, KV, FEAT]) for p in range(2)]
        v_own = [sb(f"v_own{p}", [P, KV, FEAT]) for p in range(2)]
        z_tile = [sb(f"z_tile{p}", [P, C]) for p in range(2)]
        rope_a = sb("rope_a", [P, QK_HEADS, DH])
        rope_b = sb("rope_b", [P, QK_HEADS, DH])
        roped = sb("roped", [P, QK_HEADS, DH])
        neg_max = sb("neg_max", [P, 8, GRP])
        max_rows = sb("max_rows", [P, 8, GRP, FEAT], F32R)
        probs = [sb(f"probs{i}", [P, 512]) for i in range(4)]
        o_tok = sb("o_tok", [P, 16, FEAT])
        o_inv = sb("o_inv", [P, 16])
        o_norm = sb("o_norm", [P, 16, DH])
        o_parts = sb("o_parts", [P, 16, FEAT], F32R)
        o_back = [sb(f"o_back{i}", [P, 16 * FEAT]) for i in range(2)]
        o_t = sb("o_t", [P, HALVES * REP, P], F32R)
        resid = sb("resid", [P, C])
        stats = sb("stats", [P, 6])
        mean_var = sb("mean_var", [P, 2])
        var_eps = sb("var_eps", [P, 1])
        rstd = sb("rstd", [P, 1])
        shift = sb("shift", [P, 1])
        mean_rstd = sb("mean_rstd", [P, 1])
        zT_own = sb("zT_own", [P, CC, P])

        bank = [ctx.enter_context(nc.psum_tensor(f"bank{i}", [P, 512], F32)) for i in range(8)]
        b_mix, b_qt, b_o, b_s1, b_s2 = bank[0], bank[1:3], bank[3], bank[4:6], bank[6:8]

        s = {n: sem(n) for n in (
            "consts_in", "qkv_w_in", "o_w_in", "x_in", "router_in", "xT_in0", "xT_in1",
            "const_ready", "qk_const_ready", "presets", "presets_v", "w_qkv_ready", "w_qkv_hi_ready", "w_o_hi_ready", "w_o_ready",
            "xT_hi_ready", "xT_ready", "qkv_done", "rope_terms", "rope_sum", "qk_hi_ready", "qk_lo_ready",
            "qk_dup_ready", "v_psum_read", "v_ready", "q_transposed", "k_transposed", "q_t_ready", "k_t_ready",
            "k_lead_ready", "s1_done", "max_done", "max_hi_ready", "max_rows_ready", "max_transposed",
            "q_max_ready", "s2_done", "exp_done", "pv_done", "o_tok_ready", "o_inv_ready", "o_norm_ready",
            "o_hi_ready", "o_parts_ready", "o_back_ready", "o_t_ready", "attn_done", "resid_ready", "stats_ready",
            "mean_var_ready", "rstd_step", "z_ready", "z_transposed", "zT_own_ready", "zT_hi_ready",
            "zT_lo_ready", "logits_done", "logits_ready")}

        shared.close()

        def sb(name, shape, dt=F32):
            return ctx.enter_context(nc.sbuf_tensor(name, shape, dt))

        scores_e = sb("scores_e", [P, TILES, E])
        top_val = sb("top_val", [P, TILES, 8])
        top_idx = sb("top_idx", [P, TILES, 8], U32)
        top_idx_f = sb("top_idx_f", [P, TILES, 8])
        top_rel = sb("top_rel", [P, TILES, TOPK])
        top_exp = sb("top_exp", [P, TILES, TOPK])
        top_sum = sb("top_sum", [P, TILES])
        top_inv = sb("top_inv", [P, TILES])
        top_w = sb("top_w", [P, TILES, TOPK])
        top_hot = sb("top_hot", [P, TILES, TOPK, E])
        top_hot_w = sb("top_hot_w", [P, TILES, TOPK, E])
        scores_t = sb("scores_t", [E, T])
        gate = [sb(f"gate{i}", [P, 512]) for i in range(2)]
        up = [sb(f"up{i}", [P, 512]) for i in range(2)]
        up1 = [sb(f"up1_{i}", [P, 512]) for i in range(2)]
        glu = [sb(f"glu{i}", [P, 512]) for i in range(2)]
        hid = [sb(f"hid{i}", [P, 512]) for i in range(2)]
        hid_hi = [sb(f"hid_hi{i}", [P, CC, 512], F32R) for i in range(2)]
        hid_lo = [sb(f"hid_lo{i}", [P, CC, 512], F32R) for i in range(2)]
        acc = sb("acc", [P, TILES, C])
        out_stats = sb("out_stats", [P, TILES, 6])
        out_mv = sb("out_mv", [P, TILES, 2])
        out_var = sb("out_var", [P, TILES])
        out_rstd = sb("out_rstd", [P, TILES])
        for n in ("bias_in", "w_in0", "w_in1", "w_up_hi_ready", "w_dn_hi_ready", "w_up_ready", "w_ready", "gu_free", "gu_done", "gate_ready", "up_ready",
                  "up1_ready", "glu_ready", "hid_ready", "hid_hi_ready", "hid_lo_ready", "hid_free", "y_done", "y_free",
                  "top_done", "top_rel_ready", "top_exp_ready", "top_sum_ready", "top_inv_ready", "top_w_ready",
                  "top_idx_f_ready", "hot_ready", "hot_w_ready", "scores_ready", "scores_transposed", "scores_t_ready",
                  "bias_done", "acc_ready", "out_stats_ready", "out_mv_ready", "out_var_ready", "out_rstd_ready", "out_ready", "stored"):
            s[n] = sem(n)

        def experts(eng, expert):
            expert(0, 0, 0, first=True)
            with eng.Fori(0, E // 2 - 1) as i:
                expert(2 * i + 1, i, 1)
                expert(2 * i + 2, i + 1, 0)
            expert(E - 1, E // 2 - 1, 1, last=True)

        def ffn_sync(sp):
            sp.dma_start(down_b[:, :], a["down_b"]).then_inc(s["bias_in"], 16)
            sp.dma_start(up_b[:, :, :], a["up_b"]).then_inc(s["bias_in"], 16)

            def load(e, k):
                sp.dma_start(w_up[k][:, :, :], a["w_up"].rearrange("e (c p) n -> p e c n", p=P)[:, bass.ds(e, 1), :, :]
                             .rearrange("p o c n -> p (o c) n")).then_inc(s[f"w_in{k}"], 16)
                sp.dma_start(w_dn[k][:, :, :], a["w_dn"].rearrange("e (c p) n -> p e c n", p=P)[:, bass.ds(e, 1), :, :]
                             .rearrange("p o c n -> p (o c) n")).then_inc(s[f"w_in{k}"], 16)

            load(0, 0)
            load(1, 1)
            with sp.Fori(1, E // 2) as i:
                for k in range(2):
                    sp.wait_ge(s["w_ready"], 2 * i + k - 1)
                    load(2 * i + k, k)
            out_t = out.rearrange("b (t p) c -> p (b t) c", p=P)
            for c in range(2):
                sp.wait_ge(s["out_ready"], 4 * c + 4)
                sp.dma_start(out_t[:, 4 * c:4 * c + 4, :], z_res[:, 4 * c:4 * c + 4, :]).then_inc(s["stored"], 16)
            sp.wait_ge(s["stored"], 32)

        def ffn_tensor(pe):
            def unit(e, k, c, h):
                n = 4 * e + 2 * c + h
                if c == 0 and h == 0:
                    pe.wait_ge(s["w_up_ready"], e + 1)
                pe.wait_ge(s["gu_free"], n + 1)
                for m in range(2):
                    w0 = m * D + h * P
                    i = 0
                    for kc in range(CC):
                        for w, z in ((w_up_hi, zT_hi), (w_up_lo, zT_hi), (w_up_hi, zT_lo)):
                            mm = pe.matmul(bank[2 * h + m][:, :], w[k][:, kc, w0:w0 + P], z[:, kc, c * 512:(c + 1) * 512],
                                           start=i == 0, stop=i == 3 * CC - 1)
                            i += 1
                mm.then_inc(s["gu_done"], 1)

            def down(e, k, c):
                if c == 0:
                    pe.wait_ge(s["w_ready"], e + 1)
                pe.wait_ge(s["hid_lo_ready"], 4 * e + 2 * c + 2)
                for pair in range(2):
                    pe.wait_ge(s["y_free"], 4 * e + 2 * c + pair + 1)
                    for tile in range(2):
                        t0 = (2 * pair + tile) * P
                        i = 0
                        for h in range(CC):
                            for x, w in ((hid_hi, w_dn_hi), (hid_lo, w_dn_hi), (hid_hi, w_dn_lo)):
                                mm = pe.matmul(bank[4 + 2 * c + pair][:, tile * C:(tile + 1) * C], x[c][:, h, t0:t0 + P],
                                               w[k][:, h, :], start=i == 0, stop=i == 3 * CC - 1)
                                i += 1
                    mm.then_inc(s["y_done"], 1)

            def score_bias():
                pe.wait_ge(s["scores_ready"], 1)
                pe.wait_ge(s["bias_in"], 32)
                for t in range(TILES):
                    m = pe.transpose(bank[4 + t // 4][0:E, t % 4 * P:(t % 4 + 1) * P], scores_e[:, t, :], ident[:, :])
                m.then_inc(s["scores_transposed"], 1)
                pe.wait_ge(s["scores_t_ready"], 1)
                for b in (6, 7, 4, 5):
                    for tile in range(2):
                        t = 2 * ((b - 6) % 4) + tile
                        m = pe.matmul(bank[b][:, tile * C:(tile + 1) * C], scores_t[:, t * P:(t + 1) * P], down_b[:, :],
                                      start=True, stop=True)
                    m.then_inc(s["bias_done"], 1)

            def expert(e, i, k, first=False, last=False):
                unit(e, k, 0, 0)
                unit(e, k, 0, 1)
                if first:
                    score_bias()
                else:
                    down(e - 1, 1 - k, 1)
                unit(e, k, 1, 0)
                unit(e, k, 1, 1)
                down(e, k, 0)

            pe.wait_ge(s["zT_lo_ready"], TILES)
            experts(pe, expert)
            down(E - 1, 1, 1)

        def ffn_scalar(act):
            def gelu(e, c, h, first):
                n = 4 * e + 2 * c + h
                act.wait_ge(s["gate_ready"], n + 1)
                if not (first and c == 0):
                    act.wait_ge(s["hid_ready"], n - 1)
                act.activation(glu[h][:, :], gate[h][:, :], ACT.Gelu_apprx_sigmoid).then_inc(s["glu_ready"], 1)

            def hi_of_hidden(e, c, h):
                n = 4 * e + 2 * c + h
                act.wait_ge(s["hid_ready"], n + 1)
                if not (isinstance(e, int) and e == 0):
                    act.wait_ge(s["y_done"], 4 * (e - 1) + 2 * c + 2)
                act.activation(hid_hi[c][:, h, :], hid[h][:, :], ACT.Copy).then_inc(s["hid_hi_ready"], 1)

            def split_up(e, i, k, early=False):
                act.wait_ge(s[f"w_in{k}"], 32 * i + 32)
                if not early:
                    act.wait_ge(s["gu_done"], 4 * (e - 1))
                act.activation(w_up_hi[k][:, :, :], w_up[k][:, :, :], ACT.Copy).then_inc(s["w_up_hi_ready"], 1)

            def split_down(e, k, early=False):
                if not early:
                    act.wait_ge(s["y_done"], 4 * (e - 1))
                act.activation(w_dn_hi[k][:, :, :], w_dn[k][:, :, :], ACT.Copy).then_inc(s["w_dn_hi_ready"], 1)

            def expert(e, i, k, first=False, last=False):
                for c in range(2):
                    for h in range(2):
                        gelu(e, c, h, first)
                        hi_of_hidden(e, c, h)
                        if not last and (c, h) == (0, 0):
                            split_up(e + 1, i + k, 1 - k, first)
                        if not last and (c, h) == (0, 1):
                            split_down(e + 1, 1 - k, first)

            split_up(0, 0, 0, True)
            split_down(0, 0, True)
            act.wait_ge(s["top_rel_ready"], 1)
            act.activation(top_exp[:, :, :], top_rel[:, :, :], ACT.Exp).then_inc(s["top_exp_ready"], 1)
            act.wait_ge(s["scores_transposed"], 1)
            for h in range(2):
                m = act.activation(scores_t[:, h * 512:(h + 1) * 512], bank[4 + h][0:E, :], ACT.Copy)
            m.then_inc(s["scores_t_ready"], 1)
            experts(act, expert)

        def ffn_vector(dve):
            def route_weights():
                dve.wait_ge(s["logits_ready"], TILES)
                for t in range(TILES):
                    dve.max(top_val[:, t, :], logits[:, t, :]).then_inc(s["top_done"], 1)
                dve.wait_ge(s["top_done"], TILES)
                for t in range(TILES):
                    dve.max_index(top_idx[:, t, :], top_val[:, t, :], logits[:, t, :]).then_inc(s["top_done"], 1)
                dve.tensor_tensor(top_rel[:, :, :], top_val[:, :, 0:TOPK],
                                  top_val[:, :, 0:1].broadcast_to([P, TILES, TOPK]), ALU.subtract).then_inc(s["top_rel_ready"], 1)
                dve.wait_ge(s["top_done"], 2 * TILES)
                dve.tensor_copy(top_idx_f[:, :, :], top_idx[:, :, :]).then_inc(s["top_idx_f_ready"], 1)
                dve.wait_ge(s["top_idx_f_ready"], 1)
                for r in range(TOPK):
                    m = dve.tensor_tensor(top_hot[:, :, r, :],
                                          expert_no.rearrange("p (o e) -> p o e", o=1).broadcast_to([P, TILES, E]),
                                          top_idx_f[:, :, r:r + 1].broadcast_to([P, TILES, E]), ALU.is_equal)
                m.then_inc(s["hot_ready"], 1)
                dve.wait_ge(s["top_exp_ready"], 1)
                dve.tensor_reduce(top_sum[:, :], top_exp[:, :, :], AX.X, ALU.add).then_inc(s["top_sum_ready"], 1)
                dve.wait_ge(s["top_sum_ready"], 1)
                dve.reciprocal(top_inv[:, :], top_sum[:, :]).then_inc(s["top_inv_ready"], 1)
                dve.wait_ge(s["top_inv_ready"], 1)
                dve.tensor_tensor(top_w[:, :, :], top_exp[:, :, :],
                                  top_inv[:, :].rearrange("p (t o) -> p t o", o=1).broadcast_to([P, TILES, TOPK]), ALU.mult
                                  ).then_inc(s["top_w_ready"], 1)
                dve.wait_ge(s["top_w_ready"], 1)
                dve.wait_ge(s["hot_ready"], 1)
                for r in range(TOPK):
                    m = dve.tensor_tensor(top_hot_w[:, :, r, :], top_hot[:, :, r, :],
                                          top_w[:, :, r:r + 1].broadcast_to([P, TILES, E]), ALU.mult)
                m.then_inc(s["hot_w_ready"], 1)
                dve.wait_ge(s["hot_w_ready"], 1)
                dve.tensor_reduce(scores_e[:, :, :], top_hot_w[:, :, :, :].rearrange("p t r e -> p t e r"), AX.X, ALU.add
                                  ).then_inc(s["scores_ready"], 1)

            def start_acc():
                dve.wait_ge(s["z_ready"], TILES)
                for i, b in enumerate((6, 7, 4, 5)):
                    dve.wait_ge(s["bias_done"], i + 1)
                    t = 2 * ((b - 6) % 4)
                    dve.tensor_tensor(acc[:, t:t + 2, :], bank[b][:, :].rearrange("p (t c) -> p t c", t=2), z_res[:, t:t + 2, :],
                                      ALU.add).then_inc(s["acc_ready"], 1)
                dve.wait_ge(s["acc_ready"], 4)
                dve.sem_inc(s["y_free"], 4)

            def gate_up(e, c, h, first):
                n = 4 * e + 2 * c + h
                dve.wait_ge(s["gu_done"], n + 1)
                if not (first and c == 0):
                    dve.wait_ge(s["glu_ready"], n - 1)
                dve.tensor_scalar(gate[h][:, :], bank[2 * h][:, :], up_b[:, bass.ds(e, 1), h:h + 1].rearrange("p o b -> p (o b)"),
                                  LIMIT, ALU.add, ALU.min).then_inc(s["gate_ready"], 1)
                dve.tensor_scalar(up[h][:, :], bank[2 * h + 1][:, :], up_b[:, bass.ds(e, 1), 2 + h:3 + h].rearrange("p o b -> p (o b)"),
                                  LIMIT, ALU.add, ALU.min).then_inc(s["gu_free"], 1)
                dve.wait_ge(s["gu_free"], n + 3)
                dve.tensor_scalar(up1[h][:, :], up[h][:, :], -LIMIT, 1.0, ALU.max, ALU.add).then_inc(s["up1_ready"], 1)

            def hidden(e, c, h, first=False):
                n = 4 * e + 2 * c + h
                dve.wait_ge(s["glu_ready"], n + 1)
                dve.wait_ge(s["up1_ready"], n + 1)
                if not (first and c == 0):
                    dve.wait_ge(s["hid_lo_ready"], n - 1)
                dve.tensor_tensor(hid[h][:, :], up1[h][:, :], glu[h][:, :], ALU.mult).then_inc(s["hid_ready"], 1)

            def accumulate(e, c):
                for pair in range(2):
                    m = 4 * e + 2 * c + pair
                    dve.wait_ge(s["y_done"], m + 1)
                    dve.wait_ge(s["acc_ready"], m + 1)
                    for tile in range(2):
                        t = 4 * c + 2 * pair + tile
                        i = dve.scalar_tensor_tensor(acc[:, t, :], bank[4 + 2 * c + pair][:, tile * C:(tile + 1) * C],
                                                     scores_e[:, t, bass.ds(e, 1)], acc[:, t, :], ALU.mult, ALU.add)
                    i.then_inc(s["acc_ready"], 1)
                    dve.wait_ge(s["acc_ready"], m + 5)
                    dve.sem_inc(s["y_free"], 1)

            def expert(e, i, k, first=False, last=False):
                for c in range(2):
                    for h in range(2):
                        gate_up(e, c, h, first)
                        hidden(e, c, h, first)
                        if h == 0 and not first:
                            accumulate(e - 1, c)
                        if first and (c, h) == (0, 1):
                            start_acc()

            def finish(c):
                t0 = 4 * c
                for t in range(t0, t0 + 4):
                    dve.bn_stats(out_stats[:, t, :], acc[:, t, :]).then_inc(s["out_stats_ready"], 1)
                dve.wait_ge(s["out_stats_ready"], t0 + 4)
                for t in range(t0, t0 + 4):
                    dve.bn_aggr(out_mv[:, t, :], out_stats[:, t, :]).then_inc(s["out_mv_ready"], 1)

            def apply(c):
                dve.wait_ge(s["out_rstd_ready"], c + 1)
                for t in range(4 * c, 4 * c + 4):
                    dve.tensor_scalar(z_res[:, t, :], acc[:, t, :], out_mv[:, t, 0:1], out_rstd[:, t:t + 1],
                                      ALU.subtract, ALU.mult).then_inc(s["out_ready"], 1)

            dve.sem_inc(s["gu_free"], 2)
            route_weights()
            experts(dve, expert)
            accumulate(E - 1, 0)
            finish(0)
            accumulate(E - 1, 1)
            finish(1)
            apply(0)
            apply(1)

        def ffn_gpsimd(pool):
            def lo_of_hidden(e, c, h):
                n = 4 * e + 2 * c + h
                pool.wait_ge(s["hid_hi_ready"], n + 1)
                pool.tensor_tensor(hid_lo[c][:, h, :], hid[h][:, :], hid_hi[c][:, h, :].bitcast(F32), ALU.subtract
                                   ).then_inc(s["hid_lo_ready"], 1)

            def split_up(e, k):
                pool.wait_ge(s["w_up_hi_ready"], e + 1)
                pool.tensor_tensor(w_up_lo[k][:, :, :], w_up[k][:, :, :], w_up_hi[k][:, :, :].bitcast(F32), ALU.subtract
                                   ).then_inc(s["w_up_ready"], 1)

            def split_down(e, k):
                pool.wait_ge(s["w_dn_hi_ready"], e + 1)
                pool.tensor_tensor(w_dn_lo[k][:, :, :], w_dn[k][:, :, :], w_dn_hi[k][:, :, :].bitcast(F32), ALU.subtract
                                   ).then_inc(s["w_ready"], 1)

            def expert(e, i, k, first=False, last=False):
                for c in range(2):
                    for h in range(2):
                        lo_of_hidden(e, c, h)
                        if not last and (c, h) == (0, 0):
                            split_up(e + 1, 1 - k)
                        if not last and (c, h) == (0, 1):
                            split_down(e + 1, 1 - k)

            def roots(c):
                t = slice(4 * c, 4 * c + 4)
                pool.wait_ge(s["out_mv_ready"], 4 * c + 4)
                pool.tensor_tensor(out_var[:, t], out_mv[:, t, 1], c_eps.broadcast_to([P, 4]), ALU.add
                                   ).then_inc(s["out_var_ready"], 1)
                pool.wait_ge(s["out_var_ready"], c + 1)
                pool.tensor_tensor(out_rstd[:, t], out_var[:, t], c_minus_half.broadcast_to([P, 4]), ALU.pow
                                   ).then_inc(s["out_rstd_ready"], 1)

            split_up(0, 0)
            split_down(0, 0)
            experts(pool, expert)
            roots(0)
            roots(1)

        block = ctx.enter_context(nc.Block())

        def iterations(eng, head, iteration):
            head()
            iteration(0, 0, 0, first=True, early=True)
            iteration(1, 0, 1, early=True)
            with eng.Fori(1, TILES // 2 - 1) as i:
                iteration(2 * i, i, 0)
                iteration(2 * i + 1, i, 1)
            iteration(TILES - 2, TILES // 2 - 1, 0, ahead=False)
            iteration(TILES - 1, TILES // 2 - 1, 1, front=False, ahead=False)

        @block.sync
        def _(sp):
            def load_tile(t, p):
                sp.dma_start(xT[p][:, :, :], a["x_t"].rearrange("(c p) (t n) -> p t c n", p=P, n=P)[:, t, :, :]
                             ).then_inc(s[f"xT_in{p}"], 16)

            load_tile(0, 0)
            sp.dma_start(w_qkv[:, :, :], a["w_qkv"].rearrange("(c p) n -> p c n", p=P)).then_inc(s["qkv_w_in"], 16)
            sp.dma_start(rope[:, :, :], a["c_rope"]).then_inc(s["consts_in"], 16)
            sp.dma_start(small[:, :], a["c_small"]).then_inc(s["consts_in"], 16)
            sp.dma_start(qk_const[:, :, :], a["c_qk"]).then_inc(s["consts_in"], 16)
            load_tile(1, 1)
            sp.dma_start(ident[:, :], a["c_ident"]).then_inc(s["consts_in"], 16)
            sp.dma_start(mask_f[:, :, :], a["c_mask"].rearrange("m p n -> p m n")).then_inc(s["consts_in"], 16)
            sp.dma_start(w_o[:, :, :], a["w_o"].rearrange("(j p) n -> p j n", p=P)).then_inc(s["o_w_in"], 16)
            sp.dma_start(x_res[:, :, :], a["x"].rearrange("(t p) c -> p t c", p=P)).then_inc(s["x_in"], 16)
            sp.dma_start(router[:, :, :], a["router_t"].rearrange("(c p) e -> p c e", p=P)).then_inc(s["router_in"], 16)
            sp.dma_start(router_b[:, :], a["router_b"]).then_inc(s["router_in"], 16)
            with sp.Fori(1, TILES // 2) as i:
                for p in range(2):
                    sp.wait_ge(s["xT_ready"], 2 * i + p - 1)
                    load_tile(2 * i + p, p)
            ffn_sync(sp)

        @block.tensor
        def _(pe):
            def qkv(t, p):
                pe.wait_ge(s["xT_ready"], t + 1)
                n = 0
                for c in range(CC):
                    for x, w in ((xT_hi, w_qkv_hi), (xT_lo, w_qkv_hi), (xT_hi, w_qkv_lo)):
                        m = pe.matmul(b_mix[:, 0:QKV], x[p][:, c, :], w[:, c, :], start=n == 0, stop=n == 3 * CC - 1)
                        n += 1
                m.then_inc(s["qkv_done"], 1)

            def transpose_qk(t, p):
                pe.wait_ge(s["qk_lo_ready"], t + 1)
                pe.wait_ge(s["qk_dup_ready"], t + 1)
                pe.wait_ge(s["v_psum_read"], t + 1)
                for h in range(HALVES):
                    f = HEADS + h * GRP
                    m = pe.transpose(b_mix[:, h * P:(h + 1) * P], qk_parts[p][:, f:f + GRP, :].bitcast(F32), ident[:, :])
                m.then_inc(s["k_transposed"], 1)
                for h in range(HALVES):
                    for j in range(REP):
                        f = (h * REP + j) * GRP
                        m = pe.transpose(b_qt[h][:, j * P:(j + 1) * P], qk_parts[p][:, f:f + GRP, :].bitcast(F32), ident[:, :])
                    m.then_inc(s["q_transposed"], 1)

            def scores_for_max(t, p, n, early):
                h, qt, pp = n // 4, n // 2 % 2, n % 2
                if n == 0:
                    pe.wait_ge(s["q_t_ready"], 2 * t + 2)
                    pe.wait_ge(s["k_t_ready"], t + 1)
                    pe.wait_ge(s["k_lead_ready"], t + 1)
                if not (early and n < 2):
                    pe.wait_ge(s["max_done"], 8 * t + n - 1)
                b = b_s1[n % 2]
                pe.matmul(b[:, :], ident_b[:, :], mask[:, 0, :], start=True, stop=False)
                j = h * REP + 2 * pp
                pe.matmul(b[:, :], q_t[p][:, qt, j:j + 2, :].rearrange("p j q -> p (j q)"),
                          k_t[p][:, h * GRP:(h + 1) * GRP, qt * Q:qt * Q + P], start=False, stop=True
                          ).then_inc(s["s1_done"], 1)

            def transpose_max(t, h):
                pe.wait_ge(s["max_rows_ready"], 2 * t + h + 1)
                for block in range(4):
                    m = pe.transpose(b_qt[h][:, block * P:(block + 1) * P], max_rows[:, 4 * h + block, :, :].bitcast(F32),
                                     ident[:, :])
                m.then_inc(s["max_transposed"], 1)

            def scores(t, p, n, early):
                h, qt, gp = n // 4, n // 2 % 2, n % 2
                if n % 4 == 0:
                    pe.wait_ge(s["q_max_ready"], 2 * t + h + 1)
                if not (early and n < 2):
                    pe.wait_ge(s["exp_done"], 8 * t + n - 1)
                b = b_s2[n % 2]
                pe.matmul(b[:, :], ident_b[:, :], mask[:, 1, :], start=True, stop=False)
                for g in range(2):
                    m = pe.matmul(b[:, g * 256:(g + 1) * 256], k_t[p][:, h * GRP + 2 * gp + g, qt * Q:qt * Q + P],
                                  q_max[p][:, qt, h * REP:(h + 1) * REP, :], start=False, stop=g == 1)
                m.then_inc(s["s2_done"], 1)

            def values(t, p, n, early):
                h, qt, gp = n // 4, n // 2 % 2, n % 2
                if n == 0:
                    pe.wait_ge(s["v_ready"], t + 1)
                if n % 4 == 0 and not (early and n == 0):
                    pe.wait_ge(s["o_tok_ready"], 2 * t + h)
                pe.wait_ge(s["exp_done"], 8 * t + n + 1)
                v = (v_lead, v_own)[qt][p]
                for g in range(2):
                    r = (2 * gp + g) * FEAT
                    m = pe.matmul(b_o[r:r + FEAT, qt * 256:(qt + 1) * 256], v[:, h * GRP + 2 * gp + g, :],
                                  probs[n % 4][:, g * 256:(g + 1) * 256], start=True, stop=True)
                m.then_inc(s["pv_done"], 1)

            def out_proj(t):
                pe.wait_ge(s["o_t_ready"], 2 * t + 2)
                for j in range(HALVES * REP):
                    m = pe.matmul(b_mix[:, 0:C], o_t[:, j, :], w_o3[:, j, :], start=j == 0, stop=j == HALVES * REP - 1)
                m.then_inc(s["attn_done"], 1)

            def transpose_z(t, p):
                pe.wait_ge(s["z_ready"], t + 1)
                for c in range(CC):
                    m = pe.transpose(b_qt[1][:, c * P:(c + 1) * P], z_tile[p][:, c * P:(c + 1) * P], ident[:, :])
                m.then_inc(s["z_transposed"], 1)

            def route(t):
                pe.wait_ge(s["zT_hi_ready"], t + 1)
                for c in range(CC):
                    pe.matmul(b_qt[1][:, 0:E], zT_own[:, c, :], router[:, c, :], start=c == 0, stop=False)
                pe.matmul(b_qt[1][:, 0:E], ones_row[:, :], router_b[:, :], start=False, stop=True
                          ).then_inc(s["logits_done"], 1)

            def head():
                pe.wait_ge(s["w_qkv_ready"], 1)
                qkv(0, 0)
                pe.wait_ge(s["const_ready"], 1)
                transpose_qk(0, 0)
                for n in range(8):
                    scores_for_max(0, 0, n, True)
                    if n == 4:
                        transpose_max(0, 0)
                pe.wait_ge(s["k_t_ready"], 1)
                qkv(1, 1)
                scores(0, 0, 0, True)
                scores(0, 0, 1, True)
                pe.wait_ge(s["w_o_ready"], 1)
                pe.wait_ge(s["router_in"], 32)

            def iteration(t, half_t, p, first=False, early=False, front=True, ahead=True):
                values(t, p, 0, first)
                scores(t, p, 2, first)
                transpose_max(t, 1)
                values(t, p, 1, first)
                scores(t, p, 3, first)
                values(t, p, 2, first)
                scores(t, p, 4, first)
                values(t, p, 3, first)
                scores(t, p, 5, first)
                if front:
                    transpose_qk(t + 1, 1 - p)
                if front:
                    scores_for_max(t + 1, 1 - p, 0, False)
                    scores_for_max(t + 1, 1 - p, 1, False)
                values(t, p, 4, first)
                scores(t, p, 6, first)
                if front:
                    scores_for_max(t + 1, 1 - p, 2, False)
                if not first:
                    if front:
                        pe.wait_ge(s["k_t_ready"], t + 2)
                    else:
                        pe.wait_ge(s["resid_ready"], t - 1)
                    out_proj(t - 1)
                values(t, p, 5, first)
                scores(t, p, 7, first)
                if front:
                    scores_for_max(t + 1, 1 - p, 3, False)
                values(t, p, 6, first)
                if not early:
                    transpose_z(t - 2, p)
                if front:
                    scores_for_max(t + 1, 1 - p, 4, False)
                    transpose_max(t + 1, 0)
                values(t, p, 7, first)
                if front:
                    scores_for_max(t + 1, 1 - p, 5, False)
                if not early:
                    route(t - 2)
                if front:
                    scores(t + 1, 1 - p, 0, False)
                    scores_for_max(t + 1, 1 - p, 6, False)
                if ahead:
                    if first:
                        pe.wait_ge(s["k_t_ready"], 2)
                    else:
                        pe.wait_ge(s["resid_ready"], t)
                    qkv(t + 2, p)
                if front:
                    scores(t + 1, 1 - p, 1, False)
                    if not early:
                        pe.wait_ge(s["logits_ready"], t - 1)
                    scores_for_max(t + 1, 1 - p, 7, False)

            iterations(pe, head, iteration)
            pe.wait_ge(s["logits_ready"], TILES - 2)
            transpose_z(TILES - 2, 0)
            pe.wait_ge(s["resid_ready"], TILES - 1)
            out_proj(TILES - 1)
            route(TILES - 2)
            pe.wait_ge(s["logits_ready"], TILES - 1)
            transpose_z(TILES - 1, 1)
            route(TILES - 1)
            pe.wait_ge(s["resid_ready"], TILES)
            pe.wait_ge(s["logits_ready"], TILES)
            ffn_tensor(pe)

        @block.scalar
        def _(act):
            def v_copies(t, p, early):
                act.wait_ge(s["rope_terms"], t + 1)
                if not early:
                    act.wait_ge(s["pv_done"], 8 * (t - 1))
                v = b_mix[:, C + KV * DH:QKV].rearrange("p (k d) -> p k d", d=DH)
                act.activation(v_own[p][:, :, 0:DH], v, ACT.Copy)
                act.activation(v_lead[p][Q:P, :, 0:DH], v[0:Q], ACT.Copy).then_inc(s["v_psum_read"], 1)

            def q_copies(t, p):
                for h in range(HALVES):
                    act.wait_ge(s["q_transposed"], 2 * t + h + 1)
                    act.activation(q_t[p][:, :, h * REP:(h + 1) * REP, :],
                                   b_qt[h][:, :].rearrange("p (j s q) -> p s j q", j=REP, s=2), ACT.Copy
                                   ).then_inc(s["q_t_ready"], 1)

            def exponentials(t, n, early):
                act.wait_ge(s["s2_done"], 8 * t + n + 1)
                if not (early and n < 4):
                    act.wait_ge(s["pv_done"], 8 * t + n - 3)
                act.activation(probs[n % 4][:, :], b_s2[n % 2][:, :], ACT.Exp, scale=float(DH) ** -0.5
                               ).then_inc(s["exp_done"], 1)

            def normalised(t, p):
                act.wait_ge(s["rstd_step"], ROOT_STEPS * t + ROOT_STEPS)
                act.activation(z_tile[p][:, :], resid[:, :], ACT.Identity, bias=shift[:, :], scale=rstd[:, :])
                act.activation(z_res[:, bass.ds(t, 1), :].rearrange("p o c -> p (o c)"), resid[:, :], ACT.Identity,
                               bias=shift[:, :], scale=rstd[:, :]).then_inc(s["z_ready"], 1)

            def o_copy(t, h, early):
                act.wait_ge(s["o_back_ready"], 2 * t + h + 1)
                if not early and h == 0:
                    act.wait_ge(s["attn_done"], t)
                act.activation(o_t[:, h * REP:(h + 1) * REP, :].rearrange("p j (s q) -> p j s q", s=2),
                               o_back[h][:, :].rearrange("p (s j q) -> p j s q", s=2, j=REP), ACT.Copy
                               ).then_inc(s["o_t_ready"], 1)

            def z_copies(t, tail=False):
                act.wait_ge(s["z_transposed"], t + 1)
                if tail:
                    act.wait_ge(s["zT_lo_ready"], t)
                zp = b_qt[1][:, 0:C].rearrange("p (c n) -> p c n", c=CC)
                act.activation(zT_own[:, :, :], zp, ACT.Copy).then_inc(s["zT_own_ready"], 1)
                act.activation(zT_hi[:, :, bass.ts(t, P)], zp, ACT.Copy).then_inc(s["zT_hi_ready"], 1)

            def logits_copy(t):
                act.wait_ge(s["logits_done"], t + 1)
                act.activation(logits[:, bass.ds(t, 1), :], b_qt[1][:, 0:E].rearrange("p (o e) -> p o e", o=1), ACT.Copy
                               ).then_inc(s["logits_ready"], 1)

            def front_v(t, p, first, early):
                v_copies(t, p, early)
                if not first:
                    act.wait_ge(s["v_psum_read"], t + 1)
                act.activation(v_lead[p][0:Q, :, 0:DH], (v_own[1 - p] if not first else v_zero)[Q:P, :, 0:DH], ACT.Copy
                               ).then_inc(s["v_ready"], 1)

            v_zero = v_own[1]

            def head():
                act.wait_ge(s["presets_v"], 1)
                front_v(0, 0, True, True)
                q_copies(0, 0)

            def iteration(t, half_t, p, first=False, early=False, front=True, ahead=True):
                exponentials(t, 0, first)
                exponentials(t, 1, first)
                if not first:
                    o_copy(t - 1, 1, early)
                exponentials(t, 2, first)
                if front:
                    front_v(t + 1, 1 - p, False, first)
                exponentials(t, 3, first)
                if front:
                    q_copies(t + 1, 1 - p)
                exponentials(t, 4, first)
                exponentials(t, 5, first)
                exponentials(t, 6, first)
                exponentials(t, 7, first)
                o_copy(t, 0, first)
                if not early:
                    z_copies(t - 2)
                if not first:
                    normalised(t - 1, 1 - p)
                if not early:
                    logits_copy(t - 2)

            iterations(act, head, iteration)
            o_copy(TILES - 1, 1, False)
            z_copies(TILES - 2, tail=True)
            logits_copy(TILES - 2)
            normalised(TILES - 1, 1)
            z_copies(TILES - 1, tail=True)
            logits_copy(TILES - 1)
            ffn_scalar(act)

        @block.vector
        def _(dve):
            def rope_terms(t):
                dve.wait_ge(s["qkv_done"], t + 1)
                qk = b_mix[:, 0:QK_HEADS * DH].rearrange("p (h d) -> p h d", d=DH)
                hd = DH // 2
                tab = rope[:, bass.ds(t, 1), :]

                def table(lo, n):
                    return tab[:, :, lo:lo + n].broadcast_to([P, QK_HEADS, n])

                dve.tensor_tensor(rope_a[:, :, :], qk, table(0, DH), ALU.mult)
                dve.tensor_tensor(rope_b[:, :, 0:hd], qk[:, :, hd:DH], table(DH, hd), ALU.mult)
                dve.tensor_tensor(rope_b[:, :, hd:DH], qk[:, :, 0:hd], table(DH + hd, hd), ALU.mult
                                  ).then_inc(s["rope_terms"], 1)

            def rope_qk(t, p, early):
                dve.wait_ge(s["rope_terms"], t + 1)
                if not (isinstance(t, int) and t == 0):
                    dve.wait_ge(s["qk_dup_ready"], t)
                dve.tensor_tensor(roped[:, :, :], rope_a[:, :, :], rope_b[:, :, :], ALU.add).then_inc(s["rope_sum"], 1)
                dve.wait_ge(s["rope_sum"], t + 1)
                if not early:
                    dve.wait_ge(s["q_transposed"], 2 * t - 2)
                parts = qk_parts[p]
                dve.tensor_copy(parts[:, :, 0:DH], roped[:, :, :]).then_inc(s["qk_hi_ready"], 1)
                dve.wait_ge(s["qk_hi_ready"], t + 1)
                dve.tensor_tensor(parts[:, 0:HEADS, 2 * DH:3 * DH], roped[:, 0:HEADS, :],
                                  parts[:, 0:HEADS, 0:DH].bitcast(F32), ALU.subtract)
                dve.tensor_tensor(parts[:, HEADS:QK_HEADS, DH:2 * DH], roped[:, HEADS:QK_HEADS, :],
                                  parts[:, HEADS:QK_HEADS, 0:DH].bitcast(F32), ALU.subtract).then_inc(s["qk_lo_ready"], 1)

            def k_copies(t, p, early):
                dve.wait_ge(s["k_transposed"], t + 1)
                if not early:
                    dve.wait_ge(s["s2_done"], 8 * (t - 1))
                    dve.wait_ge(s["k_lead_ready"], t)
                for h in range(HALVES):
                    m = dve.tensor_tensor(
                        k_t[p][:, h * GRP:(h + 1) * GRP, WINDOW:WINDOW + P],
                        b_mix[:, h * P:(h + 1) * P].rearrange("p (o n) -> p o n", o=1).broadcast_to([P, GRP, P]),
                        group_of.rearrange("p (g o) -> p g o", o=1).broadcast_to([P, GRP, P]), ALU.mult)
                m.then_inc(s["k_t_ready"], 1)

            def row_max(t, n):
                dve.wait_ge(s["s1_done"], 8 * t + n + 1)
                dve.tensor_reduce(neg_max[:, n, :], b_s1[n % 2][:, :].rearrange("p (g k) -> p g k", g=GRP),
                                  AX.X, ALU.max, negate=True).then_inc(s["max_done"], 1)

            def max_parts(t, h, first):
                dve.wait_ge(s["max_done"], 8 * t + 4 * h + 4)
                if not first:
                    dve.wait_ge(s["max_transposed"], 2 * t + h - 1)
                rows, value = max_rows[:, 4 * h:4 * h + 4], neg_max[:, 4 * h:4 * h + 4, :].rearrange("p n (g o) -> p n g o", o=1)
                dve.tensor_copy(rows[:, :, :, ROW_NEGMAX:ROW_NEGMAX + 1], value).then_inc(s["max_hi_ready"], 1)
                dve.wait_ge(s["max_hi_ready"], 2 * t + h + 1)
                dve.tensor_tensor(rows[:, :, :, ROW_NEGMAX + 1:ROW_NEGMAX + 2], value,
                                  rows[:, :, :, ROW_NEGMAX:ROW_NEGMAX + 1].bitcast(F32), ALU.subtract
                                  ).then_inc(s["max_rows_ready"], 1)

            def add_max(t, p, h, early):
                dve.wait_ge(s["max_transposed"], 2 * t + h + 1)
                if not early and h == 0:
                    dve.wait_ge(s["s2_done"], 8 * (t - 1))
                dve.tensor_tensor(q_max[p][:, :, h * REP:(h + 1) * REP, :],
                                  b_qt[h][:, :].rearrange("p (s j q) -> p s j q", s=2, j=REP),
                                  q_t[p][:, :, h * REP:(h + 1) * REP, :].bitcast(F32), ALU.add
                                  ).then_inc(s["q_max_ready"], 1)

            def take_values(t, h, first):
                n = 2 * t + h
                dve.wait_ge(s["pv_done"], 8 * t + 4 * h + 4)
                if not (first and h == 0):
                    dve.wait_ge(s["o_norm_ready"], n)
                dve.transpose(o_tok[:, :, :].rearrange("p b f -> p (b f)"), b_o[:, :]).then_inc(s["o_tok_ready"], 1)
                dve.wait_ge(s["o_tok_ready"], n + 1)
                dve.reciprocal(o_inv[:, :], o_tok[:, :, DH]).then_inc(s["o_inv_ready"], 1)

            def give_back(t, h, first):
                n = 2 * t + h
                dve.wait_ge(s["o_parts_ready"], n + 1)
                if not first:
                    dve.wait_ge(s["o_t_ready"], n - 1)
                dve.transpose(o_back[h][:, :], o_parts[:, :, :].rearrange("p b f -> p (b f)").bitcast(F32)
                              ).then_inc(s["o_back_ready"], 1)

            def residual(t, first):
                dve.wait_ge(s["attn_done"], t + 1)
                if not first:
                    dve.wait_ge(s["z_ready"], t)
                dve.tensor_tensor(resid[:, :], b_mix[:, 0:C], x_res[:, bass.ds(t, 1), :].rearrange("p o c -> p (o c)"), ALU.add
                                  ).then_inc(s["resid_ready"], 1)
                dve.wait_ge(s["resid_ready"], t + 1)
                dve.bn_stats(stats[:, :], resid[:, :]).then_inc(s["stats_ready"], 1)
                wait_apart(dve, s["stats_ready"], t + 1, s["x_in"], 16)
                dve.bn_aggr(mean_var[:, :], stats[:, :]).then_inc(s["mean_var_ready"], 1)

            def setup():
                dve.wait_ge(s["qkv_w_in"], 16)
                dve.tensor_copy(w_qkv_hi[:, :, :], w_qkv[:, :, :]).then_inc(s["w_qkv_hi_ready"], 1)
                dve.wait_ge(s["w_qkv_hi_ready"], 1)
                dve.tensor_tensor(w_qkv_lo[:, :, :], w_qkv[:, :, :], w_qkv_hi[:, :, :].bitcast(F32), ALU.subtract
                                  ).then_inc(s["w_qkv_ready"], 1)
                dve.wait_ge(s["consts_in"], 80)
                dve.tensor_copy(ident_b[:, :], ident[:, :])
                dve.tensor_copy(mask[:, :, :], mask_f[:, :, :]).then_inc(s["const_ready"], 1)
                dve.wait_ge(s["presets"], 1)

            def setup_late():
                dve.wait_ge(s["o_w_in"], 16)
                dve.tensor_copy(w_o_hi[:, :, :], w_o[:, :, :]).then_inc(s["w_o_hi_ready"], 1)
                dve.wait_ge(s["w_o_hi_ready"], 1)
                dve.scalar_tensor_tensor(w_o3[:, :, :], w_o_hi[:, :, :].bitcast(F32), lo_row, w_o[:, :, :],
                                         ALU.mult, ALU.add).then_inc(s["w_o_ready"], 1)
                dve.wait_ge(s["x_in"], 16)

            def head():
                setup()
                rope_terms(0)
                rope_qk(0, 0, True)
                setup_late()
                k_copies(0, 0, True)
                for n in range(8):
                    row_max(0, n)
                    if n == 3:
                        max_parts(0, 0, True)
                    if n == 5:
                        add_max(0, 0, 0, True)
                max_parts(0, 1, True)

            def iteration(t, half_t, p, first=False, early=False, front=True, ahead=True):
                if front:
                    rope_terms(t + 1)
                add_max(t, p, 1, early)
                if front:
                    rope_qk(t + 1, 1 - p, first)
                take_values(t, 0, first)
                if front:
                    k_copies(t + 1, 1 - p, first)
                    row_max(t + 1, 0)
                    row_max(t + 1, 1)
                give_back(t, 0, first)
                if front:
                    row_max(t + 1, 2)
                if not first:
                    residual(t - 1, early)
                if front:
                    row_max(t + 1, 3)
                    max_parts(t + 1, 0, False)
                    row_max(t + 1, 4)
                    add_max(t + 1, 1 - p, 0, first)
                take_values(t, 1, first)
                if front:
                    row_max(t + 1, 5)
                    row_max(t + 1, 6)
                give_back(t, 1, first)
                if front:
                    row_max(t + 1, 7)
                    max_parts(t + 1, 1, False)

            iterations(dve, head, iteration)
            residual(TILES - 1, False)
            ffn_vector(dve)

        @block.gpsimd
        def _(pool):
            def copy(to, from_, shape):
                return pool.tensor_tensor(to, from_, c_one.rearrange("p (a b) -> p a b", a=1).broadcast_to(shape), ALU.mult)

            def split_x(t, half_t, p, early):
                if not early:
                    pool.wait_ge(s["qkv_done"], t - 1)
                pool.wait_ge(s[f"xT_in{p}"], 16 * half_t + 16)
                copy(xT_hi[p][:, :, :], xT[p][:, :, :], [P, CC, P]).then_inc(s["xT_hi_ready"], 1)
                pool.wait_ge(s["xT_hi_ready"], t + 1)
                pool.tensor_tensor(xT_lo[p][:, :, :], xT[p][:, :, :], xT_hi[p][:, :, :].bitcast(F32), ALU.subtract
                                   ).then_inc(s["xT_ready"], 1)

            def duplicate_hi(t, p, early):
                if not early:
                    pool.wait_ge(s["q_transposed"], 2 * t - 2)
                pool.wait_ge(s["rope_sum"], t + 1)
                parts = qk_parts[p]
                copy(parts[:, 0:HEADS, DH:2 * DH], roped[:, 0:HEADS, :], [P, HEADS, DH])
                copy(parts[:, HEADS:QK_HEADS, 2 * DH:3 * DH], roped[:, HEADS:QK_HEADS, :], [P, KV, DH]
                     ).then_inc(s["qk_dup_ready"], 1)

            def carry_keys(t, p, early):
                if not early:
                    pool.wait_ge(s["s2_done"], 8 * (t - 1))
                pool.wait_ge(s["k_t_ready"], t)
                copy(k_t[p][:, :, 0:WINDOW], k_t[1 - p][:, :, P:P + WINDOW].bitcast(F32), [P, KV, WINDOW]
                     ).then_inc(s["k_lead_ready"], 1)

            def root(t):
                n = ROOT_STEPS * t

                def step(k, out_, x, y, op):
                    pool.tensor_tensor(out_, x, y, op).then_inc(s["rstd_step"], 1)
                    pool.wait_ge(s["rstd_step"], n + k)

                pool.wait_ge(s["mean_var_ready"], t + 1)
                step(1, var_eps[:, :], mean_var[:, 1:2], c_eps, ALU.add)
                step(2, rstd[:, :], var_eps[:, :], c_minus_half, ALU.pow)
                step(3, mean_rstd[:, :], mean_var[:, 0:1], rstd[:, :], ALU.mult)
                step(4, shift[:, :], mean_rstd[:, :], c_minus_one, ALU.mult)

            def normalise(t, h, first):
                n = 2 * t + h
                inv = o_inv[:, :].rearrange("p (b o) -> p b o", o=1).broadcast_to([P, 16, DH])
                pool.wait_ge(s["o_inv_ready"], n + 1)
                if not (first and h == 0):
                    pool.wait_ge(s["o_back_ready"], n)
                for part in (0, 2):
                    pool.tensor_tensor(o_parts[:, :, part * DH:(part + 1) * DH], o_tok[:, :, 0:DH], inv, ALU.mult)
                pool.tensor_tensor(o_norm[:, :, :], o_tok[:, :, 0:DH], inv, ALU.mult).then_inc(s["o_norm_ready"], 1)
                pool.wait_ge(s["o_norm_ready"], n + 1)
                pool.tensor_tensor(o_parts[:, :, DH:2 * DH], o_norm[:, :, :], o_parts[:, :, 0:DH].bitcast(F32), ALU.subtract
                                   ).then_inc(s["o_parts_ready"], 1)

            def lo_of_z(t):
                pool.wait_ge(s["zT_hi_ready"], t + 1)
                pool.tensor_tensor(zT_lo[:, :, bass.ts(t, P)], zT_own[:, :, :], zT_hi[:, :, bass.ts(t, P)].bitcast(F32),
                                   ALU.subtract).then_inc(s["zT_lo_ready"], 1)

            def head():
                pool.memset(ones_row[:, :], 1.0)
                for c, value in ((c_eps, EPS), (c_minus_half, -0.5), (c_minus_one, -1.0), (c_one, 1.0)):
                    pool.memset(c, value)
                for v in (*v_lead, *v_own):
                    pool.memset(v[:, :, :], 0.0)
                pool.memset(o_parts[:, :, :].bitcast(F32), 0.0)
                pool.memset(max_rows[:, :, :, :].bitcast(F32), 0.0).then_inc(s["presets"], 1)
                pool.wait_ge(s["presets"], 1)
                split_x(0, 0, 0, True)
                split_x(1, 0, 1, True)
                for v in (*v_lead, *v_own):
                    m = pool.memset(v[:, :, DH:DH + 1], 1.0)
                m.then_inc(s["presets_v"], 1)
                pool.wait_ge(s["consts_in"], 80)
                for parts in qk_parts:
                    m = pool.tensor_copy(parts[:, :, 3 * DH:FEAT], qk_const[:, :, :])
                m.then_inc(s["qk_const_ready"], 1)
                pool.tensor_copy(k_t[0][:, :, 0:WINDOW],
                                 key_pad.rearrange("p (k o) -> p k o", o=1).broadcast_to([P, KV, WINDOW])
                                 ).then_inc(s["k_lead_ready"], 1)
                duplicate_hi(0, 0, True)

            def iteration(t, half_t, p, first=False, early=False, front=True, ahead=True):
                if front:
                    carry_keys(t + 1, 1 - p, first)
                    duplicate_hi(t + 1, 1 - p, first)
                normalise(t, 0, first)
                if ahead:
                    split_x(t + 2, half_t + 1, p, False)
                if not first:
                    root(t - 1)
                normalise(t, 1, first)
                if not early:
                    lo_of_z(t - 2)

            iterations(pool, head, iteration)
            lo_of_z(TILES - 2)
            root(TILES - 1)
            lo_of_z(TILES - 1)
            ffn_gpsimd(pool)


_INPUTS = ("x", "x_t", "w_qkv", "w_o", "router_t", "router_b", "w_up", "w_dn", "up_b", "down_b",
           "c_rope", "c_ident", "c_mask", "c_small", "c_qk")


def kernel(L0_attn_x, L0_attn_wq, L0_attn_wk, L0_attn_wv, L0_attn_wo, L0_ffn_router_weight, L0_ffn_router_bias,
           L0_ffn_gate_up_proj, L0_ffn_gate_up_proj_bias, L0_ffn_down_proj, L0_ffn_down_proj_bias):
    from concourse import bacc
    from concourse.bass_utils import run_bass_kernel_spmd

    x = np.asarray(L0_attn_x)[0]
    wq = np.asarray(L0_attn_wq).reshape(C, HALVES, GRP, REP, DH).transpose(0, 1, 3, 2, 4).reshape(C, C)
    wo = np.asarray(L0_attn_wo).reshape(HALVES, GRP, REP, DH, C).transpose(0, 2, 1, 3, 4)
    wo3 = np.zeros((HALVES, REP, GRP, FEAT, C), wo.dtype)
    for r in range(3):
        wo3[:, :, :, r * DH:(r + 1) * DH] = wo
    gu = np.asarray(L0_ffn_gate_up_proj).reshape(E, C, D, 2).transpose(0, 1, 3, 2).reshape(E, C, 2 * D)
    gub = np.asarray(L0_ffn_gate_up_proj_bias).reshape(E, CC, P, 2).transpose(2, 0, 3, 1).reshape(P, E, 4)
    arrays = {
        "x": x, "x_t": x.T, "w_qkv": np.concatenate([wq, np.asarray(L0_attn_wk), np.asarray(L0_attn_wv)], 1),
        "w_o": wo3.reshape(HALVES * REP * P, C), "router_t": np.asarray(L0_ffn_router_weight).T,
        "router_b": np.asarray(L0_ffn_router_bias)[None, :], "w_up": gu, "w_dn": np.asarray(L0_ffn_down_proj),
        "up_b": gub, "down_b": np.asarray(L0_ffn_down_proj_bias), **constants(),
    }
    nc = bacc.Bacc("TRN2", target_bir_lowering=False, num_devices=1)
    arrays = {n: np.ascontiguousarray(arrays[n]) for n in _INPUTS}
    aps = {n: nc.dram_tensor("in_" + n, v.shape, mybir.dt.from_np(v.dtype), kind="ExternalInput").ap() for n, v in arrays.items()}
    out = nc.dram_tensor("out", (1, T, C), F32, kind="ExternalOutput").ap()
    build(nc, aps, out)
    r = run_bass_kernel_spmd(nc, [{"in_" + n: v for n, v in arrays.items()}], core_ids=[0])
    return r.results[0]["out"]
```

```python
from contextlib import ExitStack

import numpy as np

import concourse.bass as bass
from concourse import mybir

ALU = mybir.AluOpType
ACT = mybir.ActivationFunctionType
AX = mybir.AxisListType
F32 = mybir.dt.float32
F32R = mybir.dt.float32r
BF16 = mybir.dt.bfloat16
I32 = mybir.dt.int32
U32 = mybir.dt.uint32

T, C = 1024, 256
HEADS, KV, DH = 32, 8, 8
WINDOW = 64
REP = HEADS // KV
P = 128
TILES = T // P
Q = 64
CC = C // P
FEAT = 32
GRP = 4
HALVES = KV // GRP
ROW_NEGMAX = 3 * DH
ROW_PAD = 3 * DH + 2
NEG = -1e30
E, D, TOPK = 16, 256, 4
ALPHA, LIMIT = 1.702, 7.0
EPS = 1e-5
ROOT_STEPS = 4
QKV = C + 2 * KV * DH
QK_HEADS = HEADS + KV


def wait_apart(eng, semaphore, value, settled, settled_value):
    eng.wait_ge(settled, settled_value)
    eng.wait_ge(semaphore, value)


def constants():
    inv = (1.0 / 10000.0 ** (np.arange(0, DH, 2, dtype=np.float32) / np.float32(DH))).astype(np.float32)
    ang = np.arange(T, dtype=np.float32)[:, None] * inv[None, :]
    cos, sin = np.cos(ang).astype(np.float32), np.sin(ang).astype(np.float32)
    rope = np.concatenate([cos, cos, -sin, sin], 1).reshape(TILES, P, 2 * DH).transpose(1, 0, 2)
    ident = np.eye(P, dtype=np.float32)
    qi, ki = np.arange(Q)[:, None], np.arange(P)[None, :]
    ok = (ki <= qi + WINDOW) & (ki >= qi)
    mask = np.where(ok, 0.0, NEG).astype(np.float32)
    mask_q = np.tile(np.concatenate([mask, mask], 0), (1, GRP))
    mask_k = np.tile(mask.T, (1, 8))
    group = np.zeros((P, GRP), np.float32)
    for g in range(GRP):
        group[g * FEAT:(g + 1) * FEAT, g] = 1.0
    key_pad = np.zeros((P, KV), np.float32)
    for k in range(KV):
        key_pad[(k % GRP) * FEAT + ROW_PAD, k] = NEG
    lo_row = np.zeros((P, 1), np.float32)
    for g in range(GRP):
        lo_row[g * FEAT + 2 * DH:g * FEAT + 3 * DH] = -1.0
    small = np.concatenate([group, key_pad, lo_row, np.tile(np.arange(E, dtype=np.float32), (P, 1))], 1)
    qk_const = np.zeros((P, QK_HEADS, DH), np.float32)
    qk_const[:, :HEADS, ROW_PAD - 3 * DH] = 1.0
    qk_const[:, HEADS:, 0:2] = 1.0
    return {"c_rope": np.ascontiguousarray(rope), "c_ident": ident, "c_mask": np.stack([mask_q, mask_k]),
            "c_small": small, "c_qk": qk_const}


def build(nc, a, out):
    with ExitStack() as ctx:
        def sb(name, shape, dt=F32):
            return ctx.enter_context(nc.sbuf_tensor(name, shape, dt))

        def sem(name):
            return ctx.enter_context(nc.semaphore(name))

        rope = sb("rope", [P, TILES, 2 * DH])
        ident = sb("ident", [P, P])
        ident_b = sb("ident_b", [P, P], BF16)
        mask_f = sb("mask_f", [P, 2, 512])
        mask = sb("mask", [P, 2, 512], BF16)
        small = sb("small", [P, GRP + KV + 1 + E])
        group_of = small[:, 0:GRP]
        key_pad = small[:, GRP:GRP + KV]
        lo_row = small[:, GRP + KV:GRP + KV + 1]
        expert_no = small[:, GRP + KV + 1:GRP + KV + 1 + E]
        qk_const = sb("qk_const", [P, QK_HEADS, DH])
        x_res = sb("x_res", [P, TILES, C])
        z_res = sb("z_res", [P, TILES, C])
        zT_hi = sb("zT_hi", [P, CC, T], F32R)
        zT_lo = sb("zT_lo", [P, CC, T], F32R)
        logits = sb("logits", [P, TILES, E])
        router = sb("router", [P, CC, E])
        router_b = sb("router_b", [1, E])
        ones_row = sb("ones_row", [1, P])
        w_qkv = sb("w_qkv", [P, CC, QKV])
        w_qkv_hi = sb("w_qkv_hi", [P, CC, QKV], F32R)
        w_qkv_lo = sb("w_qkv_lo", [P, CC, QKV], F32R)
        w_o = sb("w_o", [P, HALVES * REP, C])
        w_o_hi = sb("w_o_hi", [P, HALVES * REP, C], F32R)
        w_o3 = sb("w_o3", [P, HALVES * REP, C], F32R)
        root_consts = sb("root_consts", [P, 4])
        c_eps, c_minus_half, c_minus_one, c_one = (root_consts[:, i:i + 1] for i in range(4))
        down_b = sb("down_b", [E, C])
        up_b = sb("up_b", [P, E, 4])
        w_up = [sb(f"w_up{i}", [P, CC, 2 * D]) for i in range(2)]
        w_up_hi = [sb(f"w_up_hi{i}", [P, CC, 2 * D], F32R) for i in range(2)]
        w_up_lo = [sb(f"w_up_lo{i}", [P, CC, 2 * D], F32R) for i in range(2)]
        w_dn = [sb(f"w_dn{i}", [P, CC, C]) for i in range(2)]
        w_dn_hi = [sb(f"w_dn_hi{i}", [P, CC, C], F32R) for i in range(2)]
        w_dn_lo = [sb(f"w_dn_lo{i}", [P, CC, C], F32R) for i in range(2)]
        shared = ctx.enter_context(ExitStack())

        def sb(name, shape, dt=F32):
            return shared.enter_context(nc.sbuf_tensor(name, shape, dt))

        xT = [sb(f"xT{p}", [P, CC, P]) for p in range(2)]
        xT_hi = [sb(f"xT_hi{p}", [P, CC, P], F32R) for p in range(2)]
        xT_lo = [sb(f"xT_lo{p}", [P, CC, P], F32R) for p in range(2)]
        qk_parts = [sb(f"qk_parts{p}", [P, QK_HEADS, FEAT], F32R) for p in range(2)]
        rope_a = sb("rope_a", [P, QK_HEADS, DH])
        rope_b = sb("rope_b", [P, QK_HEADS, DH])
        roped = sb("roped", [P, QK_HEADS, DH])
        neg_max = sb("neg_max", [P, 8, GRP])
        max_rows = sb("max_rows", [P, 8, GRP, FEAT], F32R)
        q_t = [sb(f"q_t{p}", [P, 2, HALVES * REP, Q], F32R) for p in range(2)]
        q_max = [sb(f"q_max{p}", [P, 2, HALVES * REP, Q], F32R) for p in range(2)]
        k_t = [sb(f"k_t{p}", [P, KV, WINDOW + P], F32R) for p in range(2)]
        v_lead = [sb(f"v_lead{p}", [P, KV, FEAT]) for p in range(2)]
        v_own = [sb(f"v_own{p}", [P, KV, FEAT]) for p in range(2)]
        probs = [sb(f"probs{i}", [P, 512]) for i in range(4)]
        z_tile = [sb(f"z_tile{p}", [P, C]) for p in range(2)]
        o_tok = sb("o_tok", [P, 16, FEAT])
        o_inv = sb("o_inv", [P, 16])
        o_norm = sb("o_norm", [P, 16, DH])
        o_parts = sb("o_parts", [P, 16, FEAT], F32R)
        o_back = [sb(f"o_back{i}", [P, 16 * FEAT]) for i in range(2)]
        o_t = sb("o_t", [P, HALVES * REP, P], F32R)
        resid = sb("resid", [P, C])
        stats = sb("stats", [P, 6])
        mean_var = sb("mean_var", [P, 2])
        var_eps = sb("var_eps", [P, 1])
        rstd = sb("rstd", [P, 1])
        shift = sb("shift", [P, 1])
        mean_rstd = sb("mean_rstd", [P, 1])
        zT_own = sb("zT_own", [P, CC, P])

        bank = [ctx.enter_context(nc.psum_tensor(f"bank{i}", [P, 512], F32)) for i in range(8)]
        b_mix, b_qt, b_o, b_s1, b_s2 = bank[0], bank[1:3], bank[3], bank[4:6], bank[6:8]

        def b_proj(t):
            return b_s1[0] if isinstance(t, int) and t >= TILES - 2 else b_mix

        def b_z(t):
            return b_s1[1] if isinstance(t, int) and t >= TILES - 3 else b_qt[1]

        s = {n: sem(n) for n in (
            "tables_in", "consts_in", "qkv_w_in", "o_w_in", "x_in", "router_in", "xT_in0", "xT_in1",
            "const_ready", "presets", "presets_v", "k_zero", "w_qkv_ready", "w_qkv_hi_ready", "w_o_hi_ready", "w_o_ready",
            "xT_hi_ready", "xT_ready", "qkv_done", "rope_terms", "rope_sum", "qk_hi_ready", "qk_lo_ready",
            "qk_dup_ready", "v_psum_read", "v_ready", "q_transposed", "k_transposed", "q_t_ready", "k_t_ready",
            "k_lead_ready", "s1_done", "max_done", "max_hi_ready", "max_rows_ready", "max_transposed",
            "q_max_ready", "s2_done", "exp_done", "pv_done", "o_tok_ready", "o_inv_ready", "o_norm_ready",
            "o_parts_ready", "o_back_ready", "o_t_ready", "attn_done", "resid_ready", "stats_ready",
            "mean_var_ready", "rstd_step", "z_ready", "z_transposed", "zT_hi_ready",
            "zT_lo_ready", "logits_done", "logits_ready")}

        shared.close()

        def sb(name, shape, dt=F32):
            return ctx.enter_context(nc.sbuf_tensor(name, shape, dt))

        gate = [sb(f"gate{i}", [P, 512]) for i in range(2)]
        up = [sb(f"up{i}", [P, 512]) for i in range(2)]
        up1 = [sb(f"up1_{i}", [P, 512]) for i in range(2)]
        glu = [sb(f"glu{i}", [P, 512]) for i in range(2)]
        hid = [sb(f"hid{i}", [P, 512]) for i in range(2)]
        hid_hi = [sb(f"hid_hi{i}", [P, CC, 512], F32R) for i in range(2)]
        hid_lo = [sb(f"hid_lo{i}", [P, CC, 512], F32R) for i in range(2)]
        scores_e = sb("scores_e", [P, TILES, E])
        top_val = sb("top_val", [P, TILES, 8])
        top_idx = sb("top_idx", [P, TILES, 8], U32)
        top_idx_f = sb("top_idx_f", [P, TILES, 8])
        top_rel = sb("top_rel", [P, TILES, TOPK])
        top_exp = sb("top_exp", [P, TILES, TOPK])
        top_sum = sb("top_sum", [P, TILES])
        top_inv = sb("top_inv", [P, TILES])
        top_w = sb("top_w", [P, TILES, TOPK])
        top_hot = sb("top_hot", [P, TILES, TOPK, E])
        top_hot_w = sb("top_hot_w", [P, TILES, TOPK, E])
        scores_t = sb("scores_t", [E, T])
        acc = sb("acc", [P, TILES, C])
        out_stats = sb("out_stats", [P, TILES, 6])
        out_mv = sb("out_mv", [P, TILES, 2])
        out_var = sb("out_var", [P, TILES])
        out_rstd = sb("out_rstd", [P, TILES])
        out_mean_rstd = sb("out_mean_rstd", [P, TILES])
        out_shift = sb("out_shift", [P, TILES])
        for n in ("bias_in", "w_in0", "w_in1", "w_up_hi_ready", "w_dn_hi_ready", "w_up_ready", "w_ready", "gu_free", "gu_done", "gate_ready",
                  "up1_ready", "glu_ready", "hid_ready", "hid_hi_ready", "hid_lo_ready", "y_done", "y_free",
                  "top_val_ready", "top_idx_ready", "top_rel_ready", "top_exp_ready", "top_sum_ready", "top_inv_ready", "top_w_ready",
                  "top_idx_f_ready", "hot_ready", "hot_w_ready", "scores_ready", "scores_transposed", "scores_t_ready",
                  "bias_done", "acc_ready", "out_stats_ready", "out_mv_ready", "out_var_ready", "out_rstd_ready",
                  "out_mean_rstd_ready", "out_shift_ready", "out_ready", "last_out_ready", "stored"):
            s[n] = sem(n)

        def experts(eng, expert):
            expert(0, 0, 0, first=True)
            with eng.Fori(0, E // 2 - 1) as i:
                expert(2 * i + 1, i, 1)
                expert(2 * i + 2, i + 1, 0)
            expert(E - 1, E // 2 - 1, 1, last=True)

        def up_hi(act, k):
            act.activation(w_up_hi[k][:, :, :], w_up[k][:, :, :], ACT.Copy).then_inc(s["w_up_hi_ready"], 1)

        def down_hi(act, k):
            act.activation(w_dn_hi[k][:, :, :], w_dn[k][:, :, :], ACT.Copy).then_inc(s["w_dn_hi_ready"], 1)

        def up_lo(pool, e, k):
            pool.wait_ge(s["w_up_hi_ready"], e + 1)
            pool.tensor_tensor(w_up_lo[k][:, :, :], w_up[k][:, :, :], w_up_hi[k][:, :, :].bitcast(F32), ALU.subtract
                               ).then_inc(s["w_up_ready"], 1)

        def down_lo(pool, e, k):
            pool.wait_ge(s["w_dn_hi_ready"], e + 1)
            pool.tensor_tensor(w_dn_lo[k][:, :, :], w_dn[k][:, :, :], w_dn_hi[k][:, :, :].bitcast(F32), ALU.subtract
                               ).then_inc(s["w_ready"], 1)

        def ffn_sync(sp):
            sp.dma_start(down_b[:, :], a["down_b"]).then_inc(s["bias_in"], 16)
            sp.dma_start(up_b[:, :, :], a["up_b"]).then_inc(s["bias_in"], 16)

            def load(e, k):
                sp.dma_start(w_up[k][:, :, :], a["w_up"].rearrange("e (c p) n -> p e c n", p=P)[:, bass.ds(e, 1), :, :]
                             .rearrange("p o c n -> p (o c) n")).then_inc(s[f"w_in{k}"], 16)
                sp.dma_start(w_dn[k][:, :, :], a["w_dn"].rearrange("e (c p) n -> p e c n", p=P)[:, bass.ds(e, 1), :, :]
                             .rearrange("p o c n -> p (o c) n")).then_inc(s[f"w_in{k}"], 16)

            load(0, 0)
            load(1, 1)
            with sp.Fori(1, E // 2) as i:
                for k in range(2):
                    sp.wait_ge(s["w_ready"], 2 * i + k - 1)
                    load(2 * i + k, k)
            out_t = out.rearrange("b (t p) c -> p (b t) c", p=P)
            stores = ((0, 4), (4, 6), (6, 8))
            for t0, t1 in stores:
                if t1 < TILES:
                    sp.wait_ge(s["out_ready"], t1)
                else:
                    sp.wait_ge(s["last_out_ready"], 2)
                sp.dma_start(out_t[:, t0:t1, :], z_res[:, t0:t1, :]).then_inc(s["stored"], 16)
            sp.wait_ge(s["stored"], 16 * len(stores))

        def unit_part(pe, k, c, h, m, kc):
            w0 = m * D + h * P
            for i, (w, z) in enumerate(((w_up_hi, zT_hi), (w_up_lo, zT_hi), (w_up_hi, zT_lo))):
                mm = pe.matmul(bank[2 * h + m][:, :], w[k][:, kc, w0:w0 + P], z[:, kc, c * 512:(c + 1) * 512],
                               start=kc == 0 and i == 0, stop=kc == CC - 1 and i == 2)
            if (m, kc) == (1, CC - 1):
                mm.then_inc(s["gu_done"], 1)

        def ffn_tensor(pe, out_proj, transpose_z, route):
            def unit(e, k, c, h):
                if c == 0 and h == 0:
                    pe.wait_ge(s["w_up_ready"], e + 1)
                pe.wait_ge(s["gu_free"], 4 * e + 2 * c + h + 1)
                for m in range(2):
                    for kc in range(CC):
                        unit_part(pe, k, c, h, m, kc)

            def down(e, k, c):
                if c == 0:
                    pe.wait_ge(s["w_ready"], e + 1)
                pe.wait_ge(s["hid_lo_ready"], 4 * e + 2 * c + 2)
                for pair in range(2):
                    pe.wait_ge(s["y_free"], 4 * e + 2 * c + pair + 1)
                    for tile in range(2):
                        t0 = (2 * pair + tile) * P
                        i = 0
                        for h in range(CC):
                            for x, w in ((hid_hi, w_dn_hi), (hid_lo, w_dn_hi), (hid_hi, w_dn_lo)):
                                mm = pe.matmul(bank[4 + 2 * c + pair][:, tile * C:(tile + 1) * C], x[c][:, h, t0:t0 + P],
                                               w[k][:, h, :], start=i == 0, stop=i == 3 * CC - 1)
                                i += 1
                    mm.then_inc(s["y_done"], 1)

            def transpose_scores():
                pe.wait_ge(s["scores_ready"], 1)
                for t in range(TILES):
                    m = pe.transpose(bank[4 + t // 4][0:E, t % 4 * P:(t % 4 + 1) * P], scores_e[:, t, :], ident[:, :])
                m.then_inc(s["scores_transposed"], 1)

            def score_bias():
                pe.wait_ge(s["bias_in"], 32)
                pe.wait_ge(s["scores_t_ready"], 1)
                for pair in range(TILES // 2):
                    for tile in range(2):
                        t = 2 * pair + tile
                        m = pe.matmul(bank[4 + pair][:, tile * C:(tile + 1) * C], scores_t[:, t * P:(t + 1) * P], down_b[:, :],
                                      start=True, stop=True)
                    m.then_inc(s["bias_done"], 1)

            def expert(e, i, k, first=False, last=False):
                if not first:
                    unit(e, k, 0, 0)
                    unit(e, k, 0, 1)
                    down(e - 1, 1 - k, 1)
                unit(e, k, 1, 0)
                if first:
                    transpose_scores()
                unit(e, k, 1, 1)
                if first:
                    score_bias()
                down(e, k, 0)

            pe.wait_ge(s["logits_ready"], TILES - 2)
            transpose_z(TILES - 2, 0)
            pe.wait_ge(s["gu_free"], 2)
            unit_part(pe, 0, 0, 1, 0, 0)
            unit_part(pe, 0, 0, 1, 0, 1)
            unit_part(pe, 0, 0, 1, 1, 0)
            pe.wait_ge(s["resid_ready"], TILES - 1)
            out_proj(TILES - 1)
            unit_part(pe, 0, 0, 1, 1, 1)
            route(TILES - 2)
            pe.wait_ge(s["logits_ready"], TILES - 1)
            transpose_z(TILES - 1, 1)
            route(TILES - 1)
            pe.wait_ge(s["zT_lo_ready"], TILES)
            experts(pe, expert)
            down(E - 1, 1, 1)

        def ffn_scalar(act):
            def gelu(e, c, h, first):
                n = 4 * e + 2 * c + h
                act.wait_ge(s["gate_ready"], n + 1)
                if not (first and c == 0):
                    act.wait_ge(s["hid_ready"], n - 1)
                act.activation(glu[h][:, :], gate[h][:, :], ACT.Gelu_apprx_sigmoid).then_inc(s["glu_ready"], 1)

            def hi_of_hidden(e, c, h):
                n = 4 * e + 2 * c + h
                act.wait_ge(s["hid_ready"], n + 1)
                if not (isinstance(e, int) and e == 0):
                    act.wait_ge(s["y_done"], 4 * (e - 1) + 2 * c + 2)
                act.activation(hid_hi[c][:, h, :], hid[h][:, :], ACT.Copy).then_inc(s["hid_hi_ready"], 1)

            def split_up(e, i, k, early=False):
                act.wait_ge(s[f"w_in{k}"], 32 * i + 32)
                if not early:
                    act.wait_ge(s["gu_done"], 4 * (e - 1))
                up_hi(act, k)

            def split_down(e, k, early=False):
                if not early:
                    act.wait_ge(s["y_done"], 4 * (e - 1))
                down_hi(act, k)

            def expert(e, i, k, first=False, last=False):
                if first:
                    gelu(e, 0, 0, first)
                    gelu(e, 0, 1, first)
                    scores_copy()
                    hi_of_hidden(e, 0, 0)
                    hi_of_hidden(e, 0, 1)
                    split_up(e + 1, i + k, 1 - k, first)
                    split_down(e + 1, 1 - k, first)
                for c in range(1 if first else 0, 2):
                    for h in range(2):
                        gelu(e, c, h, first)
                        hi_of_hidden(e, c, h)
                        if not last and (c, h) == (0, 0):
                            split_up(e + 1, i + k, 1 - k)
                        if not last and (c, h) == (0, 1):
                            split_down(e + 1, 1 - k)

            def scores_copy():
                act.wait_ge(s["scores_transposed"], 1)
                for h in range(2):
                    m = act.activation(scores_t[:, h * 512:(h + 1) * 512], bank[4 + h][0:E, :], ACT.Copy)
                m.then_inc(s["scores_t_ready"], 1)

            def apply(pair):
                act.wait_ge(s["out_shift_ready"], pair + 1)
                for t in (2 * pair, 2 * pair + 1):
                    act.activation(z_res[:, t, :], acc[:, t, :], ACT.Identity, bias=out_shift[:, t:t + 1],
                                   scale=out_rstd[:, t:t + 1]).then_inc(s["out_ready"], 1)

            act.wait_ge(s["top_rel_ready"], 1)
            act.activation(top_exp[:, :, :], top_rel[:, :, :], ACT.Exp).then_inc(s["top_exp_ready"], 1)
            experts(act, expert)
            for pair in range(TILES // 2 - 1):
                apply(pair)

        def ffn_vector(dve, residual):
            def top_logits(tiles):
                dve.wait_ge(s["logits_ready"], tiles[-1] + 1)
                for t in tiles:
                    dve.max(top_val[:, t, :], logits[:, t, :]).then_inc(s["top_val_ready"], 1)
                dve.wait_ge(s["top_val_ready"], tiles[-1] + 1)
                for t in tiles:
                    dve.max_index(top_idx[:, t, :], top_val[:, t, :], logits[:, t, :]).then_inc(s["top_idx_ready"], 1)

            def route_weights():
                dve.tensor_tensor(top_rel[:, :, :], top_val[:, :, 0:TOPK],
                                  top_val[:, :, 0:1].broadcast_to([P, TILES, TOPK]), ALU.subtract).then_inc(s["top_rel_ready"], 1)
                dve.wait_ge(s["top_idx_ready"], TILES)
                dve.tensor_copy(top_idx_f[:, :, :], top_idx[:, :, :]).then_inc(s["top_idx_f_ready"], 1)
                dve.wait_ge(s["top_idx_f_ready"], 1)
                for r in range(TOPK):
                    m = dve.tensor_tensor(top_hot[:, :, r, :],
                                          expert_no.rearrange("p (o e) -> p o e", o=1).broadcast_to([P, TILES, E]),
                                          top_idx_f[:, :, r:r + 1].broadcast_to([P, TILES, E]), ALU.is_equal)
                m.then_inc(s["hot_ready"], 1)
                dve.wait_ge(s["top_exp_ready"], 1)
                dve.tensor_reduce(top_sum[:, :], top_exp[:, :, :], AX.X, ALU.add).then_inc(s["top_sum_ready"], 1)
                dve.wait_ge(s["top_sum_ready"], 1)
                dve.reciprocal(top_inv[:, :], top_sum[:, :]).then_inc(s["top_inv_ready"], 1)
                dve.wait_ge(s["top_inv_ready"], 1)
                dve.tensor_tensor(top_w[:, :, :], top_exp[:, :, :],
                                  top_inv[:, :].rearrange("p (t o) -> p t o", o=1).broadcast_to([P, TILES, TOPK]), ALU.mult
                                  ).then_inc(s["top_w_ready"], 1)
                dve.wait_ge(s["top_w_ready"], 1)
                dve.wait_ge(s["hot_ready"], 1)
                for r in range(TOPK):
                    m = dve.tensor_tensor(top_hot_w[:, :, r, :], top_hot[:, :, r, :],
                                          top_w[:, :, r:r + 1].broadcast_to([P, TILES, E]), ALU.mult)
                m.then_inc(s["hot_w_ready"], 1)
                dve.wait_ge(s["hot_w_ready"], 1)
                dve.tensor_reduce(scores_e[:, :, :], top_hot_w[:, :, :, :].rearrange("p t r e -> p t e r"), AX.X, ALU.add
                                  ).then_inc(s["scores_ready"], 1)

            def start_acc(pair):
                dve.wait_ge(s["bias_done"], pair + 1)
                dve.tensor_tensor(acc[:, 2 * pair:2 * pair + 2, :], bank[4 + pair][:, :].rearrange("p (t c) -> p t c", t=2),
                                  z_res[:, 2 * pair:2 * pair + 2, :], ALU.add).then_inc(s["acc_ready"], 1)
                dve.wait_ge(s["acc_ready"], pair + 1)
                dve.sem_inc(s["y_free"], 1)

            def gate_up(e, c, h, first):
                n = 4 * e + 2 * c + h
                dve.wait_ge(s["gu_done"], n + 1)
                if not (first and c == 0):
                    dve.wait_ge(s["glu_ready"], n - 1)
                dve.tensor_scalar(gate[h][:, :], bank[2 * h][:, :], up_b[:, bass.ds(e, 1), h:h + 1].rearrange("p o b -> p (o b)"),
                                  LIMIT, ALU.add, ALU.min).then_inc(s["gate_ready"], 1)
                dve.tensor_scalar(up[h][:, :], bank[2 * h + 1][:, :], up_b[:, bass.ds(e, 1), 2 + h:3 + h].rearrange("p o b -> p (o b)"),
                                  LIMIT, ALU.add, ALU.min).then_inc(s["gu_free"], 1)
                dve.wait_ge(s["gu_free"], n + 3)
                dve.tensor_scalar(up1[h][:, :], up[h][:, :], -LIMIT, 1.0, ALU.max, ALU.add).then_inc(s["up1_ready"], 1)

            def hidden(e, c, h, first=False):
                n = 4 * e + 2 * c + h
                dve.wait_ge(s["glu_ready"], n + 1)
                dve.wait_ge(s["up1_ready"], n + 1)
                if not (first and c == 0):
                    dve.wait_ge(s["hid_lo_ready"], n - 1)
                dve.tensor_tensor(hid[h][:, :], up1[h][:, :], glu[h][:, :], ALU.mult).then_inc(s["hid_ready"], 1)

            def accumulate(e, c, pair):
                m = 4 * e + 2 * c + pair
                dve.wait_ge(s["y_done"], m + 1)
                dve.wait_ge(s["acc_ready"], m + 1)
                for tile in range(2):
                    t = 4 * c + 2 * pair + tile
                    i = dve.scalar_tensor_tensor(acc[:, t, :], bank[4 + 2 * c + pair][:, tile * C:(tile + 1) * C],
                                                 scores_e[:, t, bass.ds(e, 1)], acc[:, t, :], ALU.mult, ALU.add)
                i.then_inc(s["acc_ready"], 1)
                dve.wait_ge(s["acc_ready"], m + 5)
                dve.sem_inc(s["y_free"], 1)

            def expert(e, i, k, first=False, last=False):
                for c in range(2):
                    for h in range(2):
                        if first and (c, h) == (1, 1):
                            start_acc(0)
                        if not (first and c == 0):
                            gate_up(e, c, h, first)
                        if first and (c, h) == (1, 1):
                            start_acc(1)
                        hidden(e, c, h, first)
                        if not first and not (last and (c, h) == (1, 1)):
                            accumulate(e - 1, c, h)
                if first:
                    start_acc(2)
                    start_acc(3)

            def finish(pair):
                tiles = (2 * pair, 2 * pair + 1)
                for t in tiles:
                    dve.bn_stats(out_stats[:, t, :], acc[:, t, :]).then_inc(s["out_stats_ready"], 1)
                dve.wait_ge(s["out_stats_ready"], 2 * pair + 2)
                for t in tiles:
                    dve.bn_aggr(out_mv[:, t, :], out_stats[:, t, :]).then_inc(s["out_mv_ready"], 1)

            def apply_last():
                dve.wait_ge(s["out_rstd_ready"], TILES // 2)
                for t in (TILES - 2, TILES - 1):
                    dve.tensor_scalar(z_res[:, t, :], acc[:, t, :], out_mv[:, t, 0:1], out_rstd[:, t:t + 1],
                                      ALU.subtract, ALU.mult).then_inc(s["last_out_ready"], 1)

            dve.wait_ge(s["bias_in"], 32)
            gate_up(0, 0, 0, True)
            residual(TILES - 1, False)
            top_logits(range(0, TILES - 1))
            gate_up(0, 0, 1, True)
            dve.wait_ge(s["z_ready"], TILES)
            top_logits(range(TILES - 1, TILES))
            route_weights()
            experts(dve, expert)
            accumulate(E - 2, 1, 1)
            accumulate(E - 1, 0, 0)
            accumulate(E - 1, 0, 1)
            finish(0)
            finish(1)
            accumulate(E - 1, 1, 0)
            finish(2)
            accumulate(E - 1, 1, 1)
            finish(3)
            apply_last()

        def ffn_gpsimd(pool):
            def lo_of_hidden(e, c, h):
                n = 4 * e + 2 * c + h
                pool.wait_ge(s["hid_hi_ready"], n + 1)
                pool.tensor_tensor(hid_lo[c][:, h, :], hid[h][:, :], hid_hi[c][:, h, :].bitcast(F32), ALU.subtract
                                   ).then_inc(s["hid_lo_ready"], 1)

            def expert(e, i, k, first=False, last=False):
                for c in range(2):
                    for h in range(2):
                        lo_of_hidden(e, c, h)
                        if not last and not first and (c, h) == (0, 0):
                            up_lo(pool, e + 1, 1 - k)
                        if not last and not first and (c, h) == (0, 1):
                            down_lo(pool, e + 1, 1 - k)
                    if first and c == 0:
                        up_lo(pool, e + 1, 1 - k)
                        down_lo(pool, e + 1, 1 - k)

            def roots(pair):
                t = slice(2 * pair, 2 * pair + 2)
                pool.wait_ge(s["out_mv_ready"], 2 * pair + 2)
                pool.tensor_tensor(out_var[:, t], out_mv[:, t, 1], c_eps.broadcast_to([P, 2]), ALU.add
                                   ).then_inc(s["out_var_ready"], 1)
                pool.wait_ge(s["out_var_ready"], pair + 1)
                pool.tensor_tensor(out_rstd[:, t], out_var[:, t], c_minus_half.broadcast_to([P, 2]), ALU.pow
                                   ).then_inc(s["out_rstd_ready"], 1)
                if pair < TILES // 2 - 1:
                    pool.wait_ge(s["out_rstd_ready"], pair + 1)
                    pool.tensor_tensor(out_mean_rstd[:, t], out_mv[:, t, 0], out_rstd[:, t], ALU.mult
                                       ).then_inc(s["out_mean_rstd_ready"], 1)
                    pool.wait_ge(s["out_mean_rstd_ready"], pair + 1)
                    pool.tensor_tensor(out_shift[:, t], out_mean_rstd[:, t], c_minus_one.broadcast_to([P, 2]), ALU.mult
                                       ).then_inc(s["out_shift_ready"], 1)

            experts(pool, expert)
            for pair in range(TILES // 2):
                roots(pair)

        block = ctx.enter_context(nc.Block())

        def iterations(eng, head, iteration):
            head()
            iteration(0, 0, 0, first=True, early=True)
            iteration(1, 0, 1, early=True)
            with eng.Fori(1, TILES // 2 - 1) as i:
                iteration(2 * i, i, 0)
                iteration(2 * i + 1, i, 1)
            iteration(TILES - 2, TILES // 2 - 1, 0, ahead=False)
            iteration(TILES - 1, TILES // 2 - 1, 1, front=False, ahead=False)

        @block.sync
        def _(sp):
            def load_tile(t, p):
                sp.dma_start(xT[p][:, :, :], a["x_t"].rearrange("(c p) (t n) -> p t c n", p=P, n=P)[:, t, :, :]
                             ).then_inc(s[f"xT_in{p}"], 16)

            load_tile(0, 0)
            sp.dma_start(w_qkv[:, :, :], a["w_qkv"].rearrange("(c p) n -> p c n", p=P)).then_inc(s["qkv_w_in"], 16)
            sp.dma_start(rope[:, :, :], a["c_rope"]).then_inc(s["tables_in"], 16)
            sp.dma_start(small[:, :], a["c_small"]).then_inc(s["tables_in"], 16)
            sp.dma_start(qk_const[:, :, :], a["c_qk"]).then_inc(s["tables_in"], 16)
            load_tile(1, 1)
            sp.dma_start(ident[:, :], a["c_ident"]).then_inc(s["consts_in"], 16)
            sp.dma_start(mask_f[:, :, :], a["c_mask"].rearrange("m p n -> p m n")).then_inc(s["consts_in"], 16)
            sp.dma_start(w_o[:, :, :], a["w_o"].rearrange("(j p) n -> p j n", p=P)).then_inc(s["o_w_in"], 16)
            sp.dma_start(x_res[:, :, :], a["x"].rearrange("(t p) c -> p t c", p=P)).then_inc(s["x_in"], 16)
            sp.dma_start(router[:, :, :], a["router_t"].rearrange("(c p) e -> p c e", p=P)).then_inc(s["router_in"], 16)
            sp.dma_start(router_b[:, :], a["router_b"]).then_inc(s["router_in"], 16)
            with sp.Fori(1, TILES // 2) as i:
                for p in range(2):
                    sp.wait_ge(s["xT_ready"], 2 * i + p - 1)
                    load_tile(2 * i + p, p)
            ffn_sync(sp)

        @block.tensor
        def _(pe):
            def qkv(t, p):
                pe.wait_ge(s["xT_ready"], t + 1)
                n = 0
                for x, w in ((xT_hi, w_qkv_hi), (xT_lo, w_qkv_hi), (xT_hi, w_qkv_lo)):
                    if isinstance(t, int) and t == 0 and w is w_qkv_lo:
                        pe.wait_ge(s["w_qkv_ready"], 1)
                    for c in range(CC):
                        m = pe.matmul(b_mix[:, 0:QKV], x[p][:, c, :], w[:, c, :], start=n == 0, stop=n == 3 * CC - 1)
                        n += 1
                m.then_inc(s["qkv_done"], 1)

            def transpose_k(t, p):
                pe.wait_ge(s["qk_lo_ready"], t + 1)
                pe.wait_ge(s["qk_dup_ready"], t + 1)
                pe.wait_ge(s["v_psum_read"], t + 1)
                for h in range(HALVES):
                    f = HEADS + h * GRP
                    m = pe.transpose(b_mix[:, h * P:(h + 1) * P], qk_parts[p][:, f:f + GRP, :].bitcast(F32), ident[:, :])
                m.then_inc(s["k_transposed"], 1)

            def transpose_q(t, p, h):
                for j in range(REP):
                    f = (h * REP + j) * GRP
                    m = pe.transpose(b_qt[h][:, j * P:(j + 1) * P], qk_parts[p][:, f:f + GRP, :].bitcast(F32), ident[:, :])
                m.then_inc(s["q_transposed"], 1)

            def scores_for_max(t, p, n, early):
                h, qt, pp = n // 4, n // 2 % 2, n % 2
                if n % 4 == 0:
                    pe.wait_ge(s["q_t_ready"], 2 * t + h + 1)
                if n == 0:
                    pe.wait_ge(s["k_t_ready"], t + 1)
                    pe.wait_ge(s["k_lead_ready"], t + 1)
                if not (early and n < 2):
                    pe.wait_ge(s["max_done"], 8 * t + n - 1)
                b = b_s1[n % 2]
                pe.matmul(b[:, :], ident_b[:, :], mask[:, 0, :], start=True, stop=False)
                j = h * REP + 2 * pp
                pe.matmul(b[:, :], q_t[p][:, qt, j:j + 2, :].rearrange("p j q -> p (j q)"),
                          k_t[p][:, h * GRP:(h + 1) * GRP, qt * Q:qt * Q + P], start=False, stop=True
                          ).then_inc(s["s1_done"], 1)

            def transpose_max(t, h):
                pe.wait_ge(s["max_rows_ready"], 2 * t + h + 1)
                for block in range(4):
                    m = pe.transpose(b_qt[h][:, block * P:(block + 1) * P], max_rows[:, 4 * h + block, :, :].bitcast(F32),
                                     ident[:, :])
                m.then_inc(s["max_transposed"], 1)

            def scores(t, p, n, early):
                h, qt, gp = n // 4, n // 2 % 2, n % 2
                if n % 4 == 0:
                    pe.wait_ge(s["q_max_ready"], 2 * t + h + 1)
                if not (early and n < 2):
                    pe.wait_ge(s["exp_done"], 8 * t + n - 1)
                b = b_s2[n % 2]
                pe.matmul(b[:, :], ident_b[:, :], mask[:, 1, :], start=True, stop=False)
                for g in range(2):
                    m = pe.matmul(b[:, g * 256:(g + 1) * 256], k_t[p][:, h * GRP + 2 * gp + g, qt * Q:qt * Q + P],
                                  q_max[p][:, qt, h * REP:(h + 1) * REP, :], start=False, stop=g == 1)
                m.then_inc(s["s2_done"], 1)

            def values(t, p, n, early):
                h, qt, gp = n // 4, n // 2 % 2, n % 2
                if n == 0:
                    pe.wait_ge(s["v_ready"], t + 1)
                if n % 4 == 0 and not (early and n == 0):
                    pe.wait_ge(s["o_tok_ready"], 2 * t + h)
                pe.wait_ge(s["exp_done"], 8 * t + n + 1)
                v = (v_lead, v_own)[qt][p]
                for g in range(2):
                    r = (2 * gp + g) * FEAT
                    m = pe.matmul(b_o[r:r + FEAT, qt * 256:(qt + 1) * 256], v[:, h * GRP + 2 * gp + g, :],
                                  probs[n % 4][:, g * 256:(g + 1) * 256], start=True, stop=True)
                m.then_inc(s["pv_done"], 1)

            def out_proj(t):
                pe.wait_ge(s["o_t_ready"], 2 * t + 2)
                for j in range(HALVES * REP):
                    m = pe.matmul(b_proj(t)[:, 0:C], o_t[:, j, :], w_o3[:, j, :], start=j == 0, stop=j == HALVES * REP - 1)
                m.then_inc(s["attn_done"], 1)

            def transpose_z(t, p):
                pe.wait_ge(s["z_ready"], t + 1)
                for c in range(CC):
                    m = pe.transpose(b_z(t)[:, c * P:(c + 1) * P], z_tile[p][:, c * P:(c + 1) * P], ident[:, :])
                m.then_inc(s["z_transposed"], 1)

            def route(t):
                pe.wait_ge(s["zT_hi_ready"], t + 1)
                for c in range(CC):
                    pe.matmul(b_z(t)[:, 0:E], zT_own[:, c, :], router[:, c, :], start=c == 0, stop=False)
                pe.matmul(b_z(t)[:, 0:E], ones_row[:, :], router_b[:, :], start=False, stop=True
                          ).then_inc(s["logits_done"], 1)

            def head():
                pe.wait_ge(s["w_qkv_hi_ready"], 1)
                qkv(0, 0)

                pe.wait_ge(s["consts_in"], 32)
                transpose_k(0, 0)
                transpose_q(0, 0, 0)
                transpose_q(0, 0, 1)

                pe.wait_ge(s["const_ready"], 1)
                for n in range(8):
                    scores_for_max(0, 0, n, True)
                    if n == 3:
                        qkv(1, 1)
                    if n == 4:
                        transpose_max(0, 0)
                    if n > 5:
                        scores(0, 0, n - 6, True)
                transpose_max(0, 1)

            def iteration(t, half_t, p, first=False, early=False, front=True, ahead=True):
                values(t, p, 0, first)
                scores(t, p, 2, first)
                values(t, p, 1, first)
                scores(t, p, 3, first)
                if front:
                    transpose_k(t + 1, 1 - p)
                    transpose_q(t + 1, 1 - p, 0)
                if not first:
                    transpose_max(t, 1)
                values(t, p, 2, first)
                if not front:
                    pe.wait_ge(s["w_up_ready"], 1)
                    pe.wait_ge(s["zT_lo_ready"], TILES // 2)
                    pe.wait_ge(s["gu_free"], 1)
                    unit_part(pe, 0, 0, 0, 0, 0)
                scores(t, p, 4, first)
                values(t, p, 3, first)
                scores(t, p, 5, first)
                if front:
                    transpose_q(t + 1, 1 - p, 1)
                if not front:
                    unit_part(pe, 0, 0, 0, 0, 1)
                if front:
                    scores_for_max(t + 1, 1 - p, 0, False)
                    scores_for_max(t + 1, 1 - p, 1, False)
                values(t, p, 4, first)
                scores(t, p, 6, first)
                if front:
                    scores_for_max(t + 1, 1 - p, 2, False)
                if not front:
                    unit_part(pe, 0, 0, 0, 1, 0)
                if not first:
                    if front:
                        pe.wait_ge(s["k_t_ready"], t + 2)
                    if early:
                        pe.wait_ge(s["w_o_ready"], 1)
                        pe.wait_ge(s["router_in"], 32)
                    out_proj(t - 1)
                if front:
                    scores_for_max(t + 1, 1 - p, 3, False)
                values(t, p, 5, first)
                scores(t, p, 7, first)
                if not front:
                    unit_part(pe, 0, 0, 0, 1, 1)
                values(t, p, 6, first)
                if not early:
                    pe.wait_ge(s["q_t_ready"], 2 * t + (4 if front else 2))
                    transpose_z(t - 2, p)
                if front:
                    transpose_max(t + 1, 0)
                values(t, p, 7, first)
                if front:
                    scores_for_max(t + 1, 1 - p, 4, False)
                if not early:
                    route(t - 2)
                if ahead:
                    if first:
                        pe.wait_ge(s["k_t_ready"], 2)
                    else:
                        pe.wait_ge(s["resid_ready"], t)
                    qkv(t + 2, p)
                if front:
                    scores_for_max(t + 1, 1 - p, 5, False)
                    scores(t + 1, 1 - p, 0, False)
                    scores_for_max(t + 1, 1 - p, 6, False)
                    scores(t + 1, 1 - p, 1, False)
                    if not early:
                        pe.wait_ge(s["logits_ready"], t - 1)
                    scores_for_max(t + 1, 1 - p, 7, False)

            iterations(pe, head, iteration)
            ffn_tensor(pe, out_proj, transpose_z, route)

        @block.scalar
        def _(act):
            def v_copies(t, p, early):
                act.wait_ge(s["rope_terms"], t + 1)
                if not early:
                    act.wait_ge(s["pv_done"], 8 * (t - 1))
                v = b_mix[:, C + KV * DH:QKV].rearrange("p (k d) -> p k d", d=DH)
                act.activation(v_own[p][:, :, 0:DH], v, ACT.Copy)
                act.activation(v_lead[p][Q:P, :, 0:DH], v[0:Q], ACT.Copy).then_inc(s["v_psum_read"], 1)

            def k_copies(t, p, early):
                act.wait_ge(s["k_transposed"], t + 1)
                if not early:
                    act.wait_ge(s["s2_done"], 8 * (t - 1))
                    act.wait_ge(s["k_lead_ready"], t)
                for g in range(GRP):
                    rows = slice(g * FEAT, (g + 1) * FEAT)
                    m = act.activation(k_t[p][rows, g:KV:GRP, WINDOW:WINDOW + P],
                                       b_mix[rows, 0:HALVES * P].rearrange("p (h n) -> p h n", h=HALVES), ACT.Copy)
                m.then_inc(s["k_t_ready"], 1)

            def q_copy(t, p, h):
                act.wait_ge(s["q_transposed"], 2 * t + h + 1)
                act.activation(q_t[p][:, :, h * REP:(h + 1) * REP, :],
                               b_qt[h][:, :].rearrange("p (j s q) -> p s j q", j=REP, s=2), ACT.Copy
                               ).then_inc(s["q_t_ready"], 1)

            def exponentials(t, n, early):
                act.wait_ge(s["s2_done"], 8 * t + n + 1)
                if not (early and n < 4):
                    act.wait_ge(s["pv_done"], 8 * t + n - 3)
                act.activation(probs[n % 4][:, :], b_s2[n % 2][:, :], ACT.Exp, scale=float(DH) ** -0.5
                               ).then_inc(s["exp_done"], 1)

            def normalised(t, p):
                act.wait_ge(s["rstd_step"], ROOT_STEPS * t + ROOT_STEPS)
                act.activation(z_tile[p][:, :], resid[:, :], ACT.Identity, bias=shift[:, :], scale=rstd[:, :])
                act.activation(z_res[:, bass.ds(t, 1), :].rearrange("p o c -> p (o c)"), resid[:, :], ACT.Identity,
                               bias=shift[:, :], scale=rstd[:, :]).then_inc(s["z_ready"], 1)

            def o_copy(t, h, early):
                act.wait_ge(s["o_back_ready"], 2 * t + h + 1)
                if not early and h == 0:
                    act.wait_ge(s["attn_done"], t)
                act.activation(o_t[:, h * REP:(h + 1) * REP, :].rearrange("p j (s q) -> p j s q", s=2),
                               o_back[h][:, :].rearrange("p (s j q) -> p j s q", s=2, j=REP), ACT.Copy
                               ).then_inc(s["o_t_ready"], 1)

            def z_copies(t, tail=False):
                act.wait_ge(s["z_transposed"], t + 1)
                if tail:
                    act.wait_ge(s["zT_lo_ready"], t)
                zp = b_z(t)[:, 0:C].rearrange("p (c n) -> p c n", c=CC)
                act.activation(zT_own[:, :, :], zp, ACT.Copy)
                act.activation(zT_hi[:, :, bass.ts(t, P)], zp, ACT.Copy).then_inc(s["zT_hi_ready"], 1)

            def logits_copy(t):
                act.wait_ge(s["logits_done"], t + 1)
                act.activation(logits[:, bass.ds(t, 1), :], b_z(t)[:, 0:E].rearrange("p (o e) -> p o e", o=1), ACT.Copy
                               ).then_inc(s["logits_ready"], 1)

            def front_v(t, p, first, early):
                v_copies(t, p, early)
                if not first:
                    act.wait_ge(s["v_psum_read"], t + 1)
                act.activation(v_lead[p][0:Q, :, 0:DH], (v_own[1 - p] if not first else v_zero)[Q:P, :, 0:DH], ACT.Copy
                               ).then_inc(s["v_ready"], 1)

            v_zero = v_own[1]

            def head():
                act.wait_ge(s["presets_v"], 1)
                front_v(0, 0, True, True)
                act.wait_ge(s["k_zero"], 1)
                k_copies(0, 0, True)
                q_copy(0, 0, 0)
                q_copy(0, 0, 1)

            def iteration(t, half_t, p, first=False, early=False, front=True, ahead=True):
                exponentials(t, 0, first)
                exponentials(t, 1, first)
                if first:
                    front_v(1, 1, False, True)
                exponentials(t, 2, first)
                if front and not first:
                    front_v(t + 1, 1 - p, False, first)
                exponentials(t, 3, first)
                if front:
                    k_copies(t + 1, 1 - p, first)
                else:
                    down_hi(act, 0)
                if front:
                    q_copy(t + 1, 1 - p, 0)
                if not first:
                    o_copy(t - 1, 1, early)
                exponentials(t, 4, first)
                if front:
                    q_copy(t + 1, 1 - p, 1)
                exponentials(t, 5, first)
                exponentials(t, 6, first)
                if front and not ahead:
                    act.wait_ge(s["w_in0"], 32)
                    up_hi(act, 0)
                o_copy(t, 0, first)
                exponentials(t, 7, first)
                if not early:
                    z_copies(t - 2)
                if not first:
                    normalised(t - 1, 1 - p)
                if not early:
                    logits_copy(t - 2)

            iterations(act, head, iteration)
            o_copy(TILES - 1, 1, False)
            z_copies(TILES - 2, tail=True)
            logits_copy(TILES - 2)
            normalised(TILES - 1, 1)
            z_copies(TILES - 1, tail=True)
            logits_copy(TILES - 1)
            ffn_scalar(act)

        @block.vector
        def _(dve):
            def rope_terms(t):
                dve.wait_ge(s["qkv_done"], t + 1)
                qk = b_mix[:, 0:QK_HEADS * DH].rearrange("p (h d) -> p h d", d=DH)
                hd = DH // 2
                tab = rope[:, bass.ds(t, 1), :]

                def table(lo, n):
                    return tab[:, :, lo:lo + n].broadcast_to([P, QK_HEADS, n])

                dve.tensor_tensor(rope_a[:, :, :], qk, table(0, DH), ALU.mult)
                dve.tensor_tensor(rope_b[:, :, 0:hd], qk[:, :, hd:DH], table(DH, hd), ALU.mult)
                dve.tensor_tensor(rope_b[:, :, hd:DH], qk[:, :, 0:hd], table(DH + hd, hd), ALU.mult
                                  ).then_inc(s["rope_terms"], 1)

            def rope_qk(t, p, early):
                dve.wait_ge(s["rope_terms"], t + 1)
                if not (isinstance(t, int) and t == 0):
                    dve.wait_ge(s["qk_dup_ready"], t)
                dve.tensor_tensor(roped[:, :, :], rope_a[:, :, :], rope_b[:, :, :], ALU.add).then_inc(s["rope_sum"], 1)
                dve.wait_ge(s["rope_sum"], t + 1)
                if not early:
                    dve.wait_ge(s["q_transposed"], 2 * t - 2)
                parts = qk_parts[p]
                dve.tensor_copy(parts[:, :, 0:DH], roped[:, :, :]).then_inc(s["qk_hi_ready"], 1)
                dve.wait_ge(s["qk_hi_ready"], t + 1)
                dve.tensor_tensor(parts[:, 0:HEADS, 2 * DH:3 * DH], roped[:, 0:HEADS, :],
                                  parts[:, 0:HEADS, 0:DH].bitcast(F32), ALU.subtract)
                dve.tensor_tensor(parts[:, HEADS:QK_HEADS, DH:2 * DH], roped[:, HEADS:QK_HEADS, :],
                                  parts[:, HEADS:QK_HEADS, 0:DH].bitcast(F32), ALU.subtract).then_inc(s["qk_lo_ready"], 1)

            def row_max(t, n):
                dve.wait_ge(s["s1_done"], 8 * t + n + 1)
                dve.tensor_reduce(neg_max[:, n, :], b_s1[n % 2][:, :].rearrange("p (g k) -> p g k", g=GRP),
                                  AX.X, ALU.max, negate=True).then_inc(s["max_done"], 1)

            def max_parts(t, h, first):
                dve.wait_ge(s["max_done"], 8 * t + 4 * h + 4)
                if not first:
                    dve.wait_ge(s["max_transposed"], 2 * t + h - 1)
                rows, value = max_rows[:, 4 * h:4 * h + 4], neg_max[:, 4 * h:4 * h + 4, :].rearrange("p n (g o) -> p n g o", o=1)
                dve.tensor_copy(rows[:, :, :, ROW_NEGMAX:ROW_NEGMAX + 1], value).then_inc(s["max_hi_ready"], 1)
                dve.wait_ge(s["max_hi_ready"], 2 * t + h + 1)
                dve.tensor_tensor(rows[:, :, :, ROW_NEGMAX + 1:ROW_NEGMAX + 2], value,
                                  rows[:, :, :, ROW_NEGMAX:ROW_NEGMAX + 1].bitcast(F32), ALU.subtract
                                  ).then_inc(s["max_rows_ready"], 1)

            def add_max(t, p, h, early):
                dve.wait_ge(s["max_transposed"], 2 * t + h + 1)
                if not early and h == 0:
                    dve.wait_ge(s["s2_done"], 8 * (t - 1))
                dve.tensor_tensor(q_max[p][:, :, h * REP:(h + 1) * REP, :],
                                  b_qt[h][:, :].rearrange("p (s j q) -> p s j q", s=2, j=REP),
                                  q_t[p][:, :, h * REP:(h + 1) * REP, :].bitcast(F32), ALU.add
                                  ).then_inc(s["q_max_ready"], 1)

            def take_values(t, h, first):
                n = 2 * t + h
                dve.wait_ge(s["pv_done"], 8 * t + 4 * h + 4)
                if not (first and h == 0):
                    dve.wait_ge(s["o_norm_ready"], n)
                dve.transpose(o_tok[:, :, :].rearrange("p b f -> p (b f)"), b_o[:, :]).then_inc(s["o_tok_ready"], 1)
                dve.wait_ge(s["o_tok_ready"], n + 1)
                dve.reciprocal(o_inv[:, :], o_tok[:, :, DH]).then_inc(s["o_inv_ready"], 1)

            def give_back(t, h, first):
                n = 2 * t + h
                dve.wait_ge(s["o_parts_ready"], n + 1)
                if not first:
                    dve.wait_ge(s["o_t_ready"], n - 1)
                dve.transpose(o_back[h][:, :], o_parts[:, :, :].rearrange("p b f -> p (b f)").bitcast(F32)
                              ).then_inc(s["o_back_ready"], 1)

            def residual(t, first):
                dve.wait_ge(s["attn_done"], t + 1)
                if not first:
                    dve.wait_ge(s["z_ready"], t)
                dve.tensor_tensor(resid[:, :], b_proj(t)[:, 0:C], x_res[:, bass.ds(t, 1), :].rearrange("p o c -> p (o c)"), ALU.add
                                  ).then_inc(s["resid_ready"], 1)
                dve.wait_ge(s["resid_ready"], t + 1)
                dve.bn_stats(stats[:, :], resid[:, :]).then_inc(s["stats_ready"], 1)
                wait_apart(dve, s["stats_ready"], t + 1, s["x_in"], 16)
                dve.bn_aggr(mean_var[:, :], stats[:, :]).then_inc(s["mean_var_ready"], 1)

            def setup():
                dve.wait_ge(s["qkv_w_in"], 16)
                dve.tensor_copy(w_qkv_hi[:, :, :], w_qkv[:, :, :]).then_inc(s["w_qkv_hi_ready"], 1)
                dve.wait_ge(s["w_qkv_hi_ready"], 1)
                dve.tensor_tensor(w_qkv_lo[:, :, :], w_qkv[:, :, :], w_qkv_hi[:, :, :].bitcast(F32), ALU.subtract
                                  ).then_inc(s["w_qkv_ready"], 1)
                dve.wait_ge(s["tables_in"], 48)
                dve.wait_ge(s["presets"], 1)

            def setup_mask():
                dve.wait_ge(s["consts_in"], 32)
                dve.tensor_copy(ident_b[:, :], ident[:, :])
                dve.tensor_copy(mask[:, :, :], mask_f[:, :, :]).then_inc(s["const_ready"], 1)

            def split_output_weights():
                dve.wait_ge(s["o_w_in"], 16)
                dve.tensor_copy(w_o_hi[:, :, :], w_o[:, :, :]).then_inc(s["w_o_hi_ready"], 1)

            def merge_output_weights():
                dve.wait_ge(s["w_o_hi_ready"], 1)
                dve.scalar_tensor_tensor(w_o3[:, :, :], w_o_hi[:, :, :].bitcast(F32), lo_row, w_o[:, :, :],
                                         ALU.mult, ALU.add).then_inc(s["w_o_ready"], 1)

            def head():
                setup()
                rope_terms(0)
                rope_qk(0, 0, True)
                setup_mask()
                split_output_weights()
                for n in range(8):
                    row_max(0, n)
                    if n == 3:
                        max_parts(0, 0, True)
                    if n == 4:
                        add_max(0, 0, 0, True)
                max_parts(0, 1, True)
                rope_terms(1)
                rope_qk(1, 1, True)
                dve.wait_ge(s["x_in"], 16)

            def iteration(t, half_t, p, first=False, early=False, front=True, ahead=True):
                add_max(t, p, 1, early)
                if not front:
                    dve.wait_ge(s["k_t_ready"], TILES)
                    dve.sem_inc(s["gu_free"], 1)
                take_values(t, 0, first)
                if front:
                    row_max(t + 1, 0)
                    row_max(t + 1, 1)
                give_back(t, 0, first)
                if front:
                    row_max(t + 1, 2)
                    row_max(t + 1, 3)
                    max_parts(t + 1, 0, False)
                if not first:
                    residual(t - 1, early)
                else:
                    merge_output_weights()
                if front:
                    add_max(t + 1, 1 - p, 0, first)
                    row_max(t + 1, 4)
                take_values(t, 1, first)
                if front:
                    row_max(t + 1, 5)
                if ahead:
                    rope_terms(t + 2)
                if front:
                    row_max(t + 1, 6)
                if not front:
                    dve.sem_inc(s["gu_free"], 1)
                if ahead:
                    rope_qk(t + 2, p, False)
                if front:
                    row_max(t + 1, 7)
                    max_parts(t + 1, 1, False)
                give_back(t, 1, first)

            iterations(dve, head, iteration)
            ffn_vector(dve, residual)

        @block.gpsimd
        def _(pool):
            def copy(to, from_, shape):
                return pool.tensor_tensor(to, from_, c_one.rearrange("p (a b) -> p a b", a=1).broadcast_to(shape), ALU.mult)

            def split_x(t, half_t, p, early):
                if not early:
                    pool.wait_ge(s["qkv_done"], t - 1)
                pool.wait_ge(s[f"xT_in{p}"], 16 * half_t + 16)
                copy(xT_hi[p][:, :, :], xT[p][:, :, :], [P, CC, P]).then_inc(s["xT_hi_ready"], 1)
                pool.wait_ge(s["xT_hi_ready"], t + 1)
                pool.tensor_tensor(xT_lo[p][:, :, :], xT[p][:, :, :], xT_hi[p][:, :, :].bitcast(F32), ALU.subtract
                                   ).then_inc(s["xT_ready"], 1)

            def duplicate_hi(t, p, early):
                if not early:
                    pool.wait_ge(s["q_transposed"], 2 * t - 2)
                pool.wait_ge(s["rope_sum"], t + 1)
                parts = qk_parts[p]
                copy(parts[:, 0:HEADS, DH:2 * DH], roped[:, 0:HEADS, :], [P, HEADS, DH])
                copy(parts[:, HEADS:QK_HEADS, 2 * DH:3 * DH], roped[:, HEADS:QK_HEADS, :], [P, KV, DH]
                     ).then_inc(s["qk_dup_ready"], 1)

            def carry_keys(t, p, early):
                if not early:
                    pool.wait_ge(s["s2_done"], 8 * (t - 1))
                pool.wait_ge(s["k_t_ready"], t)
                copy(k_t[p][:, :, 0:WINDOW], k_t[1 - p][:, :, P:P + WINDOW].bitcast(F32), [P, KV, WINDOW]
                     ).then_inc(s["k_lead_ready"], 1)

            def root(t):
                n = ROOT_STEPS * t

                def step(k, out_, x, y, op):
                    pool.tensor_tensor(out_, x, y, op).then_inc(s["rstd_step"], 1)
                    pool.wait_ge(s["rstd_step"], n + k)

                pool.wait_ge(s["mean_var_ready"], t + 1)
                step(1, var_eps[:, :], mean_var[:, 1:2], c_eps, ALU.add)
                step(2, rstd[:, :], var_eps[:, :], c_minus_half, ALU.pow)
                step(3, mean_rstd[:, :], mean_var[:, 0:1], rstd[:, :], ALU.mult)
                step(4, shift[:, :], mean_rstd[:, :], c_minus_one, ALU.mult)

            def normalise(t, h, first):
                n = 2 * t + h
                inv = o_inv[:, :].rearrange("p (b o) -> p b o", o=1).broadcast_to([P, 16, DH])
                pool.wait_ge(s["o_inv_ready"], n + 1)
                if not (first and h == 0):
                    pool.wait_ge(s["o_back_ready"], n)
                for part in (0, 2):
                    pool.tensor_tensor(o_parts[:, :, part * DH:(part + 1) * DH], o_tok[:, :, 0:DH], inv, ALU.mult)
                pool.tensor_tensor(o_norm[:, :, :], o_tok[:, :, 0:DH], inv, ALU.mult).then_inc(s["o_norm_ready"], 1)
                pool.wait_ge(s["o_norm_ready"], n + 1)
                pool.tensor_tensor(o_parts[:, :, DH:2 * DH], o_norm[:, :, :], o_parts[:, :, 0:DH].bitcast(F32), ALU.subtract
                                   ).then_inc(s["o_parts_ready"], 1)

            def lo_of_z(t):
                pool.wait_ge(s["zT_hi_ready"], t + 1)
                pool.tensor_tensor(zT_lo[:, :, bass.ts(t, P)], zT_own[:, :, :], zT_hi[:, :, bass.ts(t, P)].bitcast(F32),
                                   ALU.subtract).then_inc(s["zT_lo_ready"], 1)

            def head():
                pool.memset(ones_row[:, :], 1.0)
                for c, value in ((c_eps, EPS), (c_minus_half, -0.5), (c_minus_one, -1.0), (c_one, 1.0)):
                    pool.memset(c, value)
                for v in (*v_lead, *v_own):
                    pool.memset(v[:, :, :], 0.0)
                pool.memset(o_parts[:, :, :].bitcast(F32), 0.0)
                pool.memset(max_rows[:, :, :, :].bitcast(F32), 0.0).then_inc(s["presets"], 1)
                pool.wait_ge(s["presets"], 1)
                split_x(0, 0, 0, True)
                for v in (*v_lead, *v_own):
                    m = pool.memset(v[:, :, DH:DH + 1], 1.0)
                m.then_inc(s["presets_v"], 1)
                for k in k_t:
                    m = pool.memset(k[:, :, :].bitcast(F32), 0.0)
                m.then_inc(s["k_zero"], 1)
                pool.wait_ge(s["k_zero"], 1)
                pool.wait_ge(s["tables_in"], 48)
                pool.tensor_copy(qk_parts[0][:, :, 3 * DH:FEAT], qk_const[:, :, :])
                duplicate_hi(0, 0, True)
                pool.tensor_copy(k_t[0][:, :, 0:WINDOW],
                                 key_pad.rearrange("p (k o) -> p k o", o=1).broadcast_to([P, KV, WINDOW])
                                 ).then_inc(s["k_lead_ready"], 1)
                pool.tensor_copy(qk_parts[1][:, :, 3 * DH:FEAT], qk_const[:, :, :])
                split_x(1, 0, 1, True)
                duplicate_hi(1, 1, True)

            def iteration(t, half_t, p, first=False, early=False, front=True, ahead=True):
                if ahead:
                    split_x(t + 2, half_t + 1, p, False)
                if front:
                    carry_keys(t + 1, 1 - p, first)
                normalise(t, 0, first)
                if front and not ahead:
                    up_lo(pool, 0, 0)
                if not first:
                    root(t - 1)
                normalise(t, 1, first)
                if not early:
                    lo_of_z(t - 2)
                if ahead:
                    duplicate_hi(t + 2, p, False)

            iterations(pool, head, iteration)
            down_lo(pool, 0, 0)
            lo_of_z(TILES - 2)
            root(TILES - 1)
            lo_of_z(TILES - 1)
            ffn_gpsimd(pool)


_INPUTS = ("x", "x_t", "w_qkv", "w_o", "router_t", "router_b", "w_up", "w_dn", "up_b", "down_b",
           "c_rope", "c_ident", "c_mask", "c_small", "c_qk")


def kernel(L0_attn_x, L0_attn_wq, L0_attn_wk, L0_attn_wv, L0_attn_wo, L0_ffn_router_weight, L0_ffn_router_bias,
           L0_ffn_gate_up_proj, L0_ffn_gate_up_proj_bias, L0_ffn_down_proj, L0_ffn_down_proj_bias):
    from concourse import bacc
    from concourse.bass_utils import run_bass_kernel_spmd

    x = np.asarray(L0_attn_x)[0]
    wq = np.asarray(L0_attn_wq).reshape(C, HALVES, GRP, REP, DH).transpose(0, 1, 3, 2, 4).reshape(C, C)
    wo = np.asarray(L0_attn_wo).reshape(HALVES, GRP, REP, DH, C).transpose(0, 2, 1, 3, 4)
    wo3 = np.zeros((HALVES, REP, GRP, FEAT, C), wo.dtype)
    for r in range(3):
        wo3[:, :, :, r * DH:(r + 1) * DH] = wo
    gu = np.asarray(L0_ffn_gate_up_proj).reshape(E, C, D, 2).transpose(0, 1, 3, 2).reshape(E, C, 2 * D)
    gub = np.asarray(L0_ffn_gate_up_proj_bias).reshape(E, CC, P, 2).transpose(2, 0, 3, 1).reshape(P, E, 4)
    arrays = {
        "x": x, "x_t": x.T, "w_qkv": np.concatenate([wq, np.asarray(L0_attn_wk), np.asarray(L0_attn_wv)], 1),
        "w_o": wo3.reshape(HALVES * REP * P, C), "router_t": np.asarray(L0_ffn_router_weight).T,
        "router_b": np.asarray(L0_ffn_router_bias)[None, :], "w_up": gu, "w_dn": np.asarray(L0_ffn_down_proj),
        "up_b": gub, "down_b": np.asarray(L0_ffn_down_proj_bias), **constants(),
    }
    nc = bacc.Bacc("TRN2", target_bir_lowering=False, num_devices=1)
    arrays = {n: np.ascontiguousarray(arrays[n]) for n in _INPUTS}
    aps = {n: nc.dram_tensor("in_" + n, v.shape, mybir.dt.from_np(v.dtype), kind="ExternalInput").ap() for n, v in arrays.items()}
    out = nc.dram_tensor("out", (1, T, C), F32, kind="ExternalOutput").ap()
    build(nc, aps, out)
    r = run_bass_kernel_spmd(nc, [{"in_" + n: v for n, v in arrays.items()}], core_ids=[0])
    return r.results[0]["out"]
```
